# Optimizing a Trainium2 kernel written in Bass

```python
import numpy as np
import jax
import jax.numpy as jnp

def _softmax(x, axis=-1):
    return jax.nn.softmax(x, axis=axis)

def _gelu(x):
    return jax.nn.gelu(x, approximate=True)

def _silu(x):
    return jax.nn.silu(x)

def _sigmoid(x):
    return jax.nn.sigmoid(x)

def _layernorm(x, axis=-1, eps=1e-05):
    m = jnp.mean(x, axis=axis, keepdims=True)
    v = jnp.var(x, axis=axis, keepdims=True)
    return (x - m) / jnp.sqrt(v + eps)

def _scatter_add(tgt, idx, src, axis=0):
    return tgt.at[idx].add(src)

def _segment_sum(src, seg, n):
    return jax.ops.segment_sum(src, seg, n)
kernel_name = 'mk_xattn_ffn_d4_seqx_r8_f945d0'

def setup_inputs(seed: int=0):
    np.random.seed(seed)
    _w = jnp.asarray

    def _rec_inputs():
        import jax
        import jax.numpy as jnp
        _rk = jax.random.key(seed)
        x = -0.0003929 + 0.9999 * jax.random.normal(jax.random.fold_in(_rk, 1), (32, 128, 128), jnp.float32)
        _lenS = 128 - jax.random.randint(jax.random.fold_in(_rk, 7), (32,), 0, max(1, 128 // 4) + 1, jnp.int32)
        _lenS2 = 128 - jax.random.randint(jax.random.fold_in(_rk, 8), (32,), 0, max(1, 128 // 4) + 1, jnp.int32)
        _ctx_768P = jax.random.normal(jax.random.fold_in(_rk, 11), (32, 16, 96), jnp.float32)
        _ctx_768c = jax.random.dirichlet(jax.random.fold_in(_rk, 511), 0.3 * jnp.ones((16,), jnp.float32), (32, 128))
        _ctx_768t = jnp.einsum('bsk,bkd->bsd', _ctx_768c, _ctx_768P)
        _ctx_768t = _ctx_768t * jax.lax.rsqrt(jnp.mean(jnp.square(_ctx_768t)) + 1e-12) * 0.953939
        ctx_768 = -7.36909e-05 + 0.999899 * (_ctx_768t + 0.3 * jax.random.normal(jax.random.fold_in(_rk, 611), (32, 128, 96), jnp.float32))
        return (x, ctx_768)
    x, ctx_768 = _rec_inputs()

    def _L0_xattn_setup():
        import jax, jax.numpy as jnp
        import numpy as np
        EPS = 1e-08
        key = jax.random.key(seed)
        kv, kt, k1, k2, k3, k4 = jax.random.split(key, 6)
        B, S = (16, 128)
        VD, TD, H = (128, 96, 64)
        visual_features = jax.random.normal(kv, (B, S, VD), dtype=jnp.float32)
        text_features = jax.random.normal(kt, (B, S, TD), dtype=jnp.float32)
        Wv = jax.random.normal(k1, (H, VD), dtype=jnp.float32) * (1.0 / np.sqrt(VD))
        bv = jax.random.normal(k2, (H,), dtype=jnp.float32) * 0.01
        Wt = jax.random.normal(k3, (H, TD), dtype=jnp.float32) * (1.0 / np.sqrt(TD))
        bt = jax.random.normal(k4, (H,), dtype=jnp.float32) * 0.01
        return {'visual_features': visual_features, 'text_features': text_features, 'Wv': Wv, 'bv': bv, 'Wt': Wt, 'bt': bt}
    _L0_xattn_all = _L0_xattn_setup()
    _L0_xattn_in = {k: v for k, v in _L0_xattn_all.items() if k in ('Wv', 'bv', 'Wt', 'bt')}
    del _L0_xattn_all

    def _L0_ffn_setup():
        import jax, jax.numpy as jnp
        import numpy as np
        B, S, H, E, I, MAX_K, A_HID = (2, 256, 128, 8, 336, 6, 50)
        key = jax.random.key(seed)
        ks = jax.random.split(key, 10)
        sc = 0.02
        return {'hidden_states': jax.random.normal(ks[0], (B, S, H), dtype=jnp.float32), 'router_w': jax.random.normal(ks[1], (E, H), dtype=jnp.float32) * sc, 'actor_w1': jax.random.normal(ks[2], (A_HID, H), dtype=jnp.float32) * sc, 'actor_b1': jnp.zeros((A_HID,), dtype=jnp.float32), 'actor_w2': jax.random.normal(ks[3], (MAX_K, A_HID), dtype=jnp.float32) * sc, 'actor_b2': jnp.zeros((MAX_K,), dtype=jnp.float32), 'gate_w': jax.random.normal(ks[4], (E, I, H), dtype=jnp.float32) * sc, 'up_w': jax.random.normal(ks[5], (E, I, H), dtype=jnp.float32) * sc, 'down_w': jax.random.normal(ks[6], (E, H, I), dtype=jnp.float32) * sc}
    _L0_ffn_all = _L0_ffn_setup()
    _L0_ffn_in = {k: v for k, v in _L0_ffn_all.items() if k in ('router_w', 'actor_w1', 'actor_b1', 'actor_w2', 'actor_b2', 'gate_w', 'up_w', 'down_w')}
    del _L0_ffn_all

    def _L1_xattn_setup():
        import jax, jax.numpy as jnp
        import numpy as np
        IMG_DIM, TXT_DIM, HID = (128, 96, 128)
        B, LQ, LK = (8, 256, 256)
        key = jax.random.key(seed)
        ks = jax.random.split(key, 8)
        s_img = 1.0 / np.sqrt(IMG_DIM)
        s_txt = 1.0 / np.sqrt(TXT_DIM)
        return {'image_features': jax.random.normal(ks[0], (B, LQ, IMG_DIM), jnp.float32), 'text_features': jax.random.normal(ks[1], (B, LK, TXT_DIM), jnp.float32), 'Wq': jax.random.uniform(ks[2], (IMG_DIM, HID), jnp.float32, -s_img, s_img), 'bq': jax.random.uniform(ks[3], (HID,), jnp.float32, -s_img, s_img), 'Wk': jax.random.uniform(ks[4], (TXT_DIM, HID), jnp.float32, -s_txt, s_txt), 'bk': jax.random.uniform(ks[5], (HID,), jnp.float32, -s_txt, s_txt), 'Wv': jax.random.uniform(ks[6], (TXT_DIM, HID), jnp.float32, -s_txt, s_txt), 'bv': jax.random.uniform(ks[7], (HID,), jnp.float32, -s_txt, s_txt)}
    _L1_xattn_all = _L1_xattn_setup()
    _L1_xattn_in = {k: v for k, v in _L1_xattn_all.items() if k in ('Wq', 'bq', 'Wk', 'bk', 'Wv', 'bv')}
    del _L1_xattn_all

    def _L1_ffn_setup():
        import jax, jax.numpy as jnp
        import numpy as np
        B, S, H, E, F = (2, 256, 128, 8, 512)
        key = jax.random.key(seed)
        k1, k2, k3, k4 = jax.random.split(key, 4)
        h = jax.random.normal(k1, (B, S, H), dtype=jnp.float32)
        Wr = jax.random.normal(k2, (H, E), dtype=jnp.float32) / np.sqrt(H)
        W1 = jax.random.normal(k3, (E, H, F), dtype=jnp.float32) / np.sqrt(H)
        W2 = jax.random.normal(k4, (E, F, H), dtype=jnp.float32) / np.sqrt(F)
        return {'h': h, 'Wr': Wr, 'W1': W1, 'W2': W2}
    _L1_ffn_all = _L1_ffn_setup()
    _L1_ffn_in = {k: v for k, v in _L1_ffn_all.items() if k in ('Wr', 'W1', 'W2')}
    del _L1_ffn_all

    def _L2_xattn_setup():
        import jax, jax.numpy as jnp
        import numpy as np
        QUERY_DIM = 128
        KEY_DIM = 96
        NUM_HEADS = 16
        HEAD_DIM = QUERY_DIM // NUM_HEADS
        SCALE = HEAD_DIM ** (-0.5)
        key = jax.random.key(seed)
        ks = jax.random.split(key, 11)
        B, Nq, Nk = (4, 512, 128)
        s_q = QUERY_DIM ** (-0.5)
        s_k = KEY_DIM ** (-0.5)
        return {'query': jax.random.normal(ks[0], (B, Nq, QUERY_DIM), jnp.float32), 'key': jax.random.normal(ks[1], (B, Nk, KEY_DIM), jnp.float32), 'value': jax.random.normal(ks[2], (B, Nk, KEY_DIM), jnp.float32), 'Wq': jax.random.normal(ks[3], (QUERY_DIM, QUERY_DIM), jnp.float32) * s_q, 'bq': jnp.zeros((QUERY_DIM,), jnp.float32), 'Wk': jax.random.normal(ks[4], (KEY_DIM, QUERY_DIM), jnp.float32) * s_k, 'bk': jnp.zeros((QUERY_DIM,), jnp.float32), 'Wv': jax.random.normal(ks[5], (KEY_DIM, QUERY_DIM), jnp.float32) * s_k, 'bv': jnp.zeros((QUERY_DIM,), jnp.float32), 'Wo': jax.random.normal(ks[6], (QUERY_DIM, QUERY_DIM), jnp.float32) * s_q, 'bo': jnp.zeros((QUERY_DIM,), jnp.float32)}
    _L2_xattn_all = _L2_xattn_setup()
    _L2_xattn_in = {k: v for k, v in _L2_xattn_all.items() if k in ('Wq', 'bq', 'Wk', 'bk', 'Wv', 'bv', 'Wo', 'bo')}
    del _L2_xattn_all

    def _L2_ffn_setup():
        import jax, jax.numpy as jnp
        import numpy as np
        B, S, D, F, E, NS, K = (2, 128, 128, 512, 8, 8, 2)
        FS = F // NS
        key = jax.random.key(seed)
        ks = jax.random.split(key, 8)
        scale = 0.02
        return {'hidden_states': jax.random.normal(ks[0], (B, S, D), jnp.float32), 'gate_W': jax.random.normal(ks[1], (E, D), jnp.float32) * scale, 'w1_e': jax.random.normal(ks[2], (E, D, F), jnp.float32) * scale, 'w3_e': jax.random.normal(ks[3], (E, D, F), jnp.float32) * scale, 'w2_e': jax.random.normal(ks[4], (E, F, D), jnp.float32) * scale, 'w1_s': jax.random.normal(ks[5], (NS, D, FS), jnp.float32) * scale, 'w3_s': jax.random.normal(ks[6], (NS, D, FS), jnp.float32) * scale, 'w2_s': jax.random.normal(ks[7], (NS, FS, D), jnp.float32) * scale}
    _L2_ffn_all = _L2_ffn_setup()
    _L2_ffn_in = {k: v for k, v in _L2_ffn_all.items() if k in ('gate_W', 'w1_e', 'w3_e', 'w2_e', 'w1_s', 'w3_s', 'w2_s')}
    del _L2_ffn_all

    def _L3_xattn_setup():
        import jax, jax.numpy as jnp
        import numpy as np
        IN_DIM = 128
        CTX_DIM = 96
        NUM_HEADS = 16
        HEAD_DIM = IN_DIM // NUM_HEADS
        SCALE = 1.0 / float(np.sqrt(HEAD_DIM))
        key = jax.random.key(seed)
        ks = jax.random.split(key, 10)
        B, NQ, NKV = (8, 128, 64)
        s_in = 1.0 / float(np.sqrt(IN_DIM))
        s_ctx = 1.0 / float(np.sqrt(CTX_DIM))
        return {'x': jax.random.normal(ks[0], (B, NQ, IN_DIM), dtype=jnp.float32), 'context': jax.random.normal(ks[1], (B, NKV, CTX_DIM), dtype=jnp.float32), 'Wq': jax.random.normal(ks[2], (IN_DIM, IN_DIM), dtype=jnp.float32) * s_in, 'bq': jax.random.normal(ks[3], (IN_DIM,), dtype=jnp.float32) * 0.01, 'Wk': jax.random.normal(ks[4], (IN_DIM, CTX_DIM), dtype=jnp.float32) * s_ctx, 'bk': jax.random.normal(ks[5], (IN_DIM,), dtype=jnp.float32) * 0.01, 'Wv': jax.random.normal(ks[6], (IN_DIM, CTX_DIM), dtype=jnp.float32) * s_ctx, 'bv': jax.random.normal(ks[7], (IN_DIM,), dtype=jnp.float32) * 0.01, 'Wo': jax.random.normal(ks[8], (IN_DIM, IN_DIM), dtype=jnp.float32) * s_in, 'bo': jax.random.normal(ks[9], (IN_DIM,), dtype=jnp.float32) * 0.01}
    _L3_xattn_all = _L3_xattn_setup()
    _L3_xattn_in = {k: v for k, v in _L3_xattn_all.items() if k in ('Wq', 'bq', 'Wk', 'bk', 'Wv', 'bv', 'Wo', 'bo')}
    del _L3_xattn_all

    def _L3_ffn_setup():
        import jax, jax.numpy as jnp
        import numpy as np
        HIDDEN = 128
        NUM_EXPERTS = 8
        TOP_K = 2
        B, S = (4, 128)
        key = jax.random.key(seed)
        ks = jax.random.split(key, 8)
        H, E = (HIDDEN, NUM_EXPERTS)
        sc = lambda fan_in: 1.0 / np.sqrt(fan_in)
        x = jax.random.normal(ks[0], (B, S, H), dtype=jnp.float32)
        Wr = jax.random.uniform(ks[1], (H, E), minval=-sc(H), maxval=sc(H), dtype=jnp.float32)
        br = jax.random.uniform(ks[2], (E,), minval=-sc(H), maxval=sc(H), dtype=jnp.float32)
        W1 = jax.random.uniform(ks[3], (E, H, 2 * H), minval=-sc(H), maxval=sc(H), dtype=jnp.float32)
        b1 = jax.random.uniform(ks[4], (E, 2 * H), minval=-sc(H), maxval=sc(H), dtype=jnp.float32)
        W2 = jax.random.uniform(ks[5], (E, 2 * H, H), minval=-sc(2 * H), maxval=sc(2 * H), dtype=jnp.float32)
        b2 = jax.random.uniform(ks[6], (E, H), minval=-sc(2 * H), maxval=sc(2 * H), dtype=jnp.float32)
        return {'x': x, 'Wr': Wr, 'br': br, 'W1': W1, 'b1': b1, 'W2': W2, 'b2': b2}
    _L3_ffn_all = _L3_ffn_setup()
    _L3_ffn_in = {k: v for k, v in _L3_ffn_all.items() if k in ('Wr', 'br', 'W1', 'b1', 'W2', 'b2')}
    del _L3_ffn_all
    return {'x': x, 'ctx_768': ctx_768, 'L0_xattn_Wv': _L0_xattn_in['Wv'], 'L0_xattn_bv': _L0_xattn_in['bv'], 'L0_xattn_Wt': _L0_xattn_in['Wt'], 'L0_xattn_bt': _L0_xattn_in['bt'], 'L0_ffn_router_w': _L0_ffn_in['router_w'], 'L0_ffn_actor_w1': _L0_ffn_in['actor_w1'], 'L0_ffn_actor_b1': _L0_ffn_in['actor_b1'], 'L0_ffn_actor_w2': _L0_ffn_in['actor_w2'], 'L0_ffn_actor_b2': _L0_ffn_in['actor_b2'], 'L0_ffn_gate_w': _L0_ffn_in['gate_w'], 'L0_ffn_up_w': _L0_ffn_in['up_w'], 'L0_ffn_down_w': _L0_ffn_in['down_w'], 'L1_xattn_Wq': _L1_xattn_in['Wq'], 'L1_xattn_bq': _L1_xattn_in['bq'], 'L1_xattn_Wk': _L1_xattn_in['Wk'], 'L1_xattn_bk': _L1_xattn_in['bk'], 'L1_xattn_Wv': _L1_xattn_in['Wv'], 'L1_xattn_bv': _L1_xattn_in['bv'], 'L1_ffn_Wr': _L1_ffn_in['Wr'], 'L1_ffn_W1': _L1_ffn_in['W1'], 'L1_ffn_W2': _L1_ffn_in['W2'], 'L2_xattn_Wq': _L2_xattn_in['Wq'], 'L2_xattn_bq': _L2_xattn_in['bq'], 'L2_xattn_Wk': _L2_xattn_in['Wk'], 'L2_xattn_bk': _L2_xattn_in['bk'], 'L2_xattn_Wv': _L2_xattn_in['Wv'], 'L2_xattn_bv': _L2_xattn_in['bv'], 'L2_xattn_Wo': _L2_xattn_in['Wo'], 'L2_xattn_bo': _L2_xattn_in['bo'], 'L2_ffn_gate_W': _L2_ffn_in['gate_W'], 'L2_ffn_w1_e': _L2_ffn_in['w1_e'], 'L2_ffn_w3_e': _L2_ffn_in['w3_e'], 'L2_ffn_w2_e': _L2_ffn_in['w2_e'], 'L2_ffn_w1_s': _L2_ffn_in['w1_s'], 'L2_ffn_w3_s': _L2_ffn_in['w3_s'], 'L2_ffn_w2_s': _L2_ffn_in['w2_s'], 'L3_xattn_Wq': _L3_xattn_in['Wq'], 'L3_xattn_bq': _L3_xattn_in['bq'], 'L3_xattn_Wk': _L3_xattn_in['Wk'], 'L3_xattn_bk': _L3_xattn_in['bk'], 'L3_xattn_Wv': _L3_xattn_in['Wv'], 'L3_xattn_bv': _L3_xattn_in['bv'], 'L3_xattn_Wo': _L3_xattn_in['Wo'], 'L3_xattn_bo': _L3_xattn_in['bo'], 'L3_ffn_Wr': _L3_ffn_in['Wr'], 'L3_ffn_br': _L3_ffn_in['br'], 'L3_ffn_W1': _L3_ffn_in['W1'], 'L3_ffn_b1': _L3_ffn_in['b1'], 'L3_ffn_W2': _L3_ffn_in['W2'], 'L3_ffn_b2': _L3_ffn_in['b2']}

def reference(x, ctx_768, L0_xattn_Wv, L0_xattn_bv, L0_xattn_Wt, L0_xattn_bt, L0_ffn_router_w, L0_ffn_actor_w1, L0_ffn_actor_b1, L0_ffn_actor_w2, L0_ffn_actor_b2, L0_ffn_gate_w, L0_ffn_up_w, L0_ffn_down_w, L1_xattn_Wq, L1_xattn_bq, L1_xattn_Wk, L1_xattn_bk, L1_xattn_Wv, L1_xattn_bv, L1_ffn_Wr, L1_ffn_W1, L1_ffn_W2, L2_xattn_Wq, L2_xattn_bq, L2_xattn_Wk, L2_xattn_bk, L2_xattn_Wv, L2_xattn_bv, L2_xattn_Wo, L2_xattn_bo, L2_ffn_gate_W, L2_ffn_w1_e, L2_ffn_w3_e, L2_ffn_w2_e, L2_ffn_w1_s, L2_ffn_w3_s, L2_ffn_w2_s, L3_xattn_Wq, L3_xattn_bq, L3_xattn_Wk, L3_xattn_bk, L3_xattn_Wv, L3_xattn_bv, L3_xattn_Wo, L3_xattn_bo, L3_ffn_Wr, L3_ffn_br, L3_ffn_W1, L3_ffn_b1, L3_ffn_W2, L3_ffn_b2):
    import jax
    import jax.numpy as jnp

    def _L0_xattn_ref(visual_features, text_features, Wv, bv, Wt, bt):
        import jax, jax.numpy as jnp
        import numpy as np
        EPS = 1e-08
        v = jnp.einsum('bsd,hd->bsh', visual_features, Wv) + bv
        t = jnp.einsum('bsd,hd->bsh', text_features, Wt) + bt
        dots = jnp.einsum('bih,bjh->bij', v, t)
        vn = jnp.linalg.norm(v, axis=-1)
        tn = jnp.linalg.norm(t, axis=-1)
        denom = jnp.maximum(vn[:, :, None] * tn[:, None, :], EPS)
        return dots / denom

    def _L0_ffn_ref(hidden_states, router_w, actor_w1, actor_b1, actor_w2, actor_b2, gate_w, up_w, down_w):
        import jax, jax.numpy as jnp
        import numpy as np
        B, S, H, E, I, MAX_K, A_HID = (2, 256, 128, 8, 336, 6, 50)
        probs = jax.nn.softmax(jnp.einsum('bsh,eh->bse', hidden_states, router_w).astype(jnp.float32), axis=-1)
        a_h = jax.nn.gelu(jnp.einsum('bsh,ah->bsa', hidden_states, actor_w1) + actor_b1)
        actor_logits = jnp.clip(jnp.einsum('bsa,ka->bsk', a_h, actor_w2) + actor_b2, -30.0, 30.0)
        sampled_k = jnp.argmax(actor_logits, axis=-1) + 1
        order = jnp.argsort(-probs, axis=-1)
        rank = jnp.argsort(order, axis=-1)
        mask = rank < sampled_k[..., None]
        scores = jnp.where(mask, probs, 0.0).astype(hidden_states.dtype)
        out = jnp.zeros_like(hidden_states)
        for e in range(E):
            g = jnp.einsum('bsh,ih->bsi', hidden_states, gate_w[e])
            u = jnp.einsum('bsh,ih->bsi', hidden_states, up_w[e])
            y = jnp.einsum('bsi,hi->bsh', jax.nn.silu(g) * u, down_w[e])
            out = out + scores[..., e:e + 1] * y
        return out

    def _L1_xattn_ref(image_features, text_features, Wq, bq, Wk, bk, Wv, bv):
        import jax, jax.numpy as jnp
        import numpy as np
        IMG_DIM, TXT_DIM, HID = (128, 96, 128)
        B, LQ, LK = (8, 256, 256)
        query = jnp.einsum('bqi,ih->bqh', image_features, Wq) + bq
        key = jnp.einsum('bkt,th->bkh', text_features, Wk) + bk
        value = jnp.einsum('bkt,th->bkh', text_features, Wv) + bv
        scale = 1.0 / jnp.sqrt(jnp.asarray(HID, query.dtype))
        scores = jnp.einsum('bqh,bkh->bqk', query, key) * scale
        weights = jax.nn.softmax(scores, axis=-1)
        attended = jnp.einsum('bqk,bkh->bqh', weights, value)
        return attended

    def _L1_ffn_ref(h, Wr, W1, W2):
        import jax, jax.numpy as jnp
        import numpy as np
        B, S, H, E, F = (2, 256, 128, 8, 512)
        g = jax.nn.softmax(h @ Wr, axis=-1)
        top2_w, top2_idx = jax.lax.top_k(g, 2)
        top2_w = top2_w / jnp.sum(top2_w, axis=-1, keepdims=True)
        hid = jax.nn.relu(jnp.einsum('bsh,ehf->bsef', h, W1))
        expert_out = jnp.einsum('bsef,efh->bseh', hid, W2)
        top2_out = jnp.take_along_axis(expert_out, top2_idx[..., None], axis=2)
        return jnp.sum(top2_out * top2_w[..., None], axis=2)

    def _L2_xattn_ref(query, key, value, Wq, bq, Wk, bk, Wv, bv, Wo, bo):
        import jax, jax.numpy as jnp
        import numpy as np
        QUERY_DIM = 128
        KEY_DIM = 96
        NUM_HEADS = 16
        HEAD_DIM = QUERY_DIM // NUM_HEADS
        SCALE = HEAD_DIM ** (-0.5)
        B, Nq, _ = query.shape
        Nk = key.shape[1]
        q = (query @ Wq + bq).reshape(B, Nq, NUM_HEADS, HEAD_DIM).transpose(0, 2, 1, 3)
        k = (key @ Wk + bk).reshape(B, Nk, NUM_HEADS, HEAD_DIM).transpose(0, 2, 1, 3)
        v = (value @ Wv + bv).reshape(B, Nk, NUM_HEADS, HEAD_DIM).transpose(0, 2, 1, 3)
        attn = jnp.einsum('bhqd,bhkd->bhqk', q, k) * SCALE
        attn = jax.nn.softmax(attn, axis=-1)
        out = jnp.einsum('bhqk,bhkd->bhqd', attn, v)
        out = out.transpose(0, 2, 1, 3).reshape(B, Nq, QUERY_DIM)
        return out @ Wo + bo

    def _L2_ffn_ref(hidden_states, gate_W, w1_e, w3_e, w2_e, w1_s, w3_s, w2_s):
        import jax, jax.numpy as jnp
        import numpy as np
        B, S, D, F, E, NS, K = (2, 128, 128, 512, 8, 8, 2)
        FS = F // NS
        b, s, d = hidden_states.shape
        e = gate_W.shape[0]
        flat = hidden_states.reshape(-1, d)
        T = flat.shape[0]
        logits = (flat @ gate_W.T).astype(jnp.float32)
        probs = jax.nn.softmax(logits, axis=-1)
        top_v, top_i = jax.lax.top_k(probs, K)
        gates = jnp.zeros((T, e), probs.dtype).at[jnp.arange(T)[:, None], top_i].set(top_v)
        g = jax.nn.silu(jnp.einsum('td,edf->etf', flat, w1_e))
        u = jnp.einsum('td,edf->etf', flat, w3_e)
        out_e = jnp.einsum('etf,efd->etd', g * u, w2_e)
        routed = jnp.einsum('te,etd->td', gates, out_e).reshape(b, s, d)
        gs = jax.nn.silu(jnp.einsum('bsd,ndf->nbsf', hidden_states, w1_s))
        us = jnp.einsum('bsd,ndf->nbsf', hidden_states, w3_s)
        shared = jnp.einsum('nbsf,nfd->bsd', gs * us, w2_s) / w1_s.shape[0]
        alpha = 0.5
        return alpha * shared + (1.0 - alpha) * routed

    def _L3_xattn_ref(x, context, Wq, bq, Wk, bk, Wv, bv, Wo, bo):
        import jax, jax.numpy as jnp
        import numpy as np
        IN_DIM = 128
        CTX_DIM = 96
        NUM_HEADS = 16
        HEAD_DIM = IN_DIM // NUM_HEADS
        SCALE = 1.0 / float(np.sqrt(HEAD_DIM))
        q = x @ Wq.T + bq
        k = context @ Wk.T + bk
        v = context @ Wv.T + bv
        B, NQ, _ = q.shape
        NKV = k.shape[1]
        q = q.reshape(B, NQ, NUM_HEADS, HEAD_DIM)
        k = k.reshape(B, NKV, NUM_HEADS, HEAD_DIM)
        v = v.reshape(B, NKV, NUM_HEADS, HEAD_DIM)
        attn = jnp.einsum('bihd,bjhd->bhij', q, k) * SCALE
        attn = jax.nn.softmax(attn, axis=-1)
        out = jnp.einsum('bhij,bjhd->bihd', attn, v)
        out = out.reshape(B, NQ, IN_DIM)
        return out @ Wo.T + bo

    def _L3_ffn_ref(x, Wr, br, W1, b1, W2, b2):
        import jax, jax.numpy as jnp
        import numpy as np
        HIDDEN = 128
        NUM_EXPERTS = 8
        TOP_K = 2
        B, S = (4, 128)
        B_, S_, H = x.shape
        xf = x.reshape(-1, H)
        logits = xf @ Wr + br
        topk_w, topk_idx = jax.lax.top_k(logits, TOP_K)
        topk_w = jax.nn.softmax(topk_w, axis=-1)
        gate = jnp.sum(jax.nn.one_hot(topk_idx, NUM_EXPERTS, dtype=xf.dtype) * topk_w[..., None], axis=1)
        h = jax.nn.relu(jnp.einsum('th,ehf->etf', xf, W1) + b1[:, None, :])
        y = jnp.einsum('etf,efh->eth', h, W2) + b2[:, None, :]
        out = jnp.einsum('te,eth->th', gate, y)
        return out.reshape(B_, S_, H)
    x = x + _L0_xattn_ref(_layernorm(x, axis=-1), ctx_768, L0_xattn_Wv, L0_xattn_bv, L0_xattn_Wt, L0_xattn_bt)
    x = x + _L0_ffn_ref(_layernorm(x, axis=-1), L0_ffn_router_w, L0_ffn_actor_w1, L0_ffn_actor_b1, L0_ffn_actor_w2, L0_ffn_actor_b2, L0_ffn_gate_w, L0_ffn_up_w, L0_ffn_down_w)
    x = x + _L1_xattn_ref(_layernorm(x, axis=-1), ctx_768, L1_xattn_Wq, L1_xattn_bq, L1_xattn_Wk, L1_xattn_bk, L1_xattn_Wv, L1_xattn_bv)
    x = x + _L1_ffn_ref(_layernorm(x, axis=-1), L1_ffn_Wr, L1_ffn_W1, L1_ffn_W2)
    x = x + _L2_xattn_ref(_layernorm(x, axis=-1), ctx_768, ctx_768, L2_xattn_Wq, L2_xattn_bq, L2_xattn_Wk, L2_xattn_bk, L2_xattn_Wv, L2_xattn_bv, L2_xattn_Wo, L2_xattn_bo)
    x = x + _L2_ffn_ref(_layernorm(x, axis=-1), L2_ffn_gate_W, L2_ffn_w1_e, L2_ffn_w3_e, L2_ffn_w2_e, L2_ffn_w1_s, L2_ffn_w3_s, L2_ffn_w2_s)
    x = x + _L3_xattn_ref(_layernorm(x, axis=-1), ctx_768, L3_xattn_Wq, L3_xattn_bq, L3_xattn_Wk, L3_xattn_bk, L3_xattn_Wv, L3_xattn_bv, L3_xattn_Wo, L3_xattn_bo)
    x = x + _L3_ffn_ref(_layernorm(x, axis=-1), L3_ffn_Wr, L3_ffn_br, L3_ffn_W1, L3_ffn_b1, L3_ffn_W2, L3_ffn_b2)
    return x

_drawn_inputs = setup_inputs


def setup_inputs(seed=0):
    import zlib

    import numpy as np

    out = dict(_drawn_inputs(seed))
    spreads = {'L0_ffn_actor_b1': (0.0, 0.8),
     'L0_ffn_actor_b2': (0.0, 0.8),
     'L2_xattn_bq': (0.0, 0.377),
     'L2_xattn_bk': (0.0, 2.0),
     'L2_xattn_bv': (0.0, 0.1),
     'L2_xattn_bo': (0.0, 0.1)}
    factors = {'L0_xattn_bv': 6.657,
     'L0_xattn_bt': 8.0,
     'L0_ffn_router_w': 5.035,
     'L0_ffn_actor_w1': 8.0,
     'L0_ffn_actor_w2': 8.0,
     'L0_ffn_gate_w': 5.769,
     'L0_ffn_up_w': 4.471,
     'L0_ffn_down_w': 4.229,
     'L1_xattn_bq': 5.071,
     'L1_xattn_bk': 64.0,
     'L2_ffn_gate_W': 8.0,
     'L2_ffn_w1_e': 8.0,
     'L2_ffn_w3_e': 8.0,
     'L2_ffn_w2_e': 8.0,
     'L2_ffn_w1_s': 8.0,
     'L2_ffn_w3_s': 8.0,
     'L2_ffn_w2_s': 8.0,
     'L3_xattn_bq': 58.723,
     'L3_xattn_bk': 64.0,
     'L3_xattn_bv': 6.202,
     'L3_xattn_bo': 13.242,
     'L3_ffn_b1': 5.45,
     'L3_ffn_b2': 3.044,
     'L3_ffn_br': 3.397}
    for name, (base, spread) in spreads.items():
        noise = np.random.default_rng([zlib.crc32(name.encode()), seed]).standard_normal(out[name].shape)
        drawn = base * np.exp(spread * noise) if base else spread * noise
        out[name] = jnp.asarray(drawn.astype(out[name].dtype))
    for name, factor in factors.items():
        out[name] = (out[name] * factor).astype(out[name].dtype)
    return out
```

```python
from contextlib import ExitStack

import concourse.bass as bass
from concourse import mybir

ALU = mybir.AluOpType
ACT = mybir.ActivationFunctionType
AX = mybir.AxisListType
F32 = mybir.dt.float32

P = 128
GROUPS = 8
T = 4
N = T * P
C = 96
EXPERTS = 8
LAYERS = 4
HEADS, HD = 16, 8
QUADS = T * 4
HID0 = 64
ACTOR, MAX_K = 50, 6
LN_EPS, COS_EPS = 1e-5, 1e-8
GELU_A, GELU_C = 0.7978845608028654, 0.044715

ROWS = [112, 128, 128, 128]
PER_UNIT = [3, 4, 4, 2]
UNITS = [8, 8, 9, 8]
GATED = [True, False, True, False]
CHUNKS = [a * b for a, b in zip(PER_UNIT, UNITS)]
LAG = 2
HRING = 4
BANKS = 4

NORM2 = [7, 7, 24, 24]
PRE_LEN = [NORM2[0] + 8, NORM2[1] + 6, NORM2[2] + 6, NORM2[3] + 9]
GATE_SCALE = [0.5, 1.0, 0.25, 1.0]
SHARED_GATE = 0.5 * 0.5 / 8


class Signal:

    def __init__(self, sem, per, credit=0):
        self.sem, self.credit = sem, credit
        self.per = [per] * LAYERS if isinstance(per, int) else list(per)
        self.base = [GROUPS * sum(self.per[:L]) for L in range(LAYERS)]

    def at(self, layer, g, k):
        return g * self.per[layer] + (self.base[layer] + self.credit + k)


def build(nc, d, out):
    with ExitStack() as ctx:
        def sb(name, shape):
            return ctx.enter_context(nc.sbuf_tensor(name, shape, F32))

        def bank(name):
            return ctx.enter_context(nc.psum_tensor(name, [P, N], F32))

        def semaphore(name):
            return ctx.enter_context(nc.semaphore(name))

        signals = []

        def signal(name, per, credit=0):
            s = Signal(semaphore(name), per, credit)
            signals.append(s)
            return s

        x = sb("x", [P, GROUPS, T, P])
        const = sb("const", [P, P + 4 + 64 + MAX_K])
        ident = const[:, 0:P]
        head_mask = const[:, P:P + 4]
        before = const[:, P + 4:P + 68].rearrange("p (e j) -> p e j", j=EXPERTS)
        iota1 = const[:, P + 68:P + 68 + MAX_K]
        ones = sb("ones", [P, P])
        half = sb("half", [P, 16])
        eps = sb("eps", [P, T])
        wg = {0: sb("wg0", [P, CHUNKS[0], ROWS[0]]), 1: sb("w1_1", [P, CHUNKS[1], P]),
              2: sb("wg2", [P, CHUNKS[2], P])}
        wu = {0: sb("wu0", [P, CHUNKS[0], ROWS[0]]), 2: sb("wu2", [P, CHUNKS[2], P])}
        wd = {0: sb("wd0", [ROWS[0], CHUNKS[0], P]), 1: sb("wd1", [P, CHUNKS[1], P]),
              2: sb("wd2", [P, CHUNKS[2], P])}
        wg[3] = wg[0].rearrange("p c r -> p (c r)")[:, 0:CHUNKS[3] * P].rearrange("p (c r) -> p c r", r=P) \
            if hasattr(wg[0], "rearrange") else wg[0][:, :, :].rearrange("p c r -> p (c r)")[:, 0:CHUNKS[3] * P] \
            .rearrange("p (c r) -> p c r", r=P)
        wd[3] = wu[0][:, :, :].rearrange("p c r -> p (c r)")[:, 0:CHUNKS[3] * P] \
            .rearrange("p (c r) -> p c r", r=P)
        b1_3 = sb("b1_3", [P, CHUNKS[3]])
        wv0 = sb("wv0", [P, HID0])
        wt0 = sb("wt0", [C + 1, HID0])
        wq = sb("wq", [P, 3, P])
        wk = sb("wk", [C + 1, 3, P])
        wv = sb("wv", [C + 1, 3, P])
        wo = sb("wo", [P, 2, P])
        bo = sb("bo", [P, 2, P])
        bv0 = sb("bv0", [HID0, 1])
        bq = sb("bq", [P, 3])
        bqs = sb("bqs", [P, 3])
        wr = sb("wr", [P, 4, EXPERTS])
        br3 = sb("br3", [P, EXPERTS])
        aw1 = sb("aw1", [P, ACTOR])
        ab1 = sb("ab1", [ACTOR, 1])
        aw2 = sb("aw2", [ACTOR, MAX_K])
        ab2 = sb("ab2", [P, MAX_K])
        b2_3 = sb("b2_3", [T * EXPERTS, T, P])
        ctxT = sb("ctxT", [C + 1, N])
        stats = sb("stats", [P, T, 6])
        moments = sb("moments", [P, T, 2])
        vare = sb("vare", [P, T])
        rstd = sb("rstd", [P, T])
        xn = sb("xn", [P, T, P])
        xnT = sb("xnT", [P, N])
        x2T = sb("x2T", [P, 2, N])
        qT = sb("qT", [P, N])
        kbd = sb("kbd", [P, T, N])
        kT = kbd[:, 0, :]
        va = sb("va", [P, T, HEADS, HD + 1])
        val = kbd[:, 1, :].rearrange("p (t d) -> p t d", t=T)
        nmax = sb("nmax", [P, 2, T])
        prob = sb("prob", [P, 2, T, P])
        probT = sb("probT", [P, 2, T, P])
        sums = sb("sums", [P, T])
        rsum = sb("rsum", [P, HEADS])
        ao = sb("ao", [P, T, P])
        aoT = sb("aoT", [P, N])
        tmp = sb("tmp", [P, T, P])
        lg = sb("lg", [P, T, EXPERTS])
        nlmax = sb("nlmax", [P, T])
        dl = sb("dl", [P, T, EXPERTS])
        ex = sb("ex", [P, T, EXPERTS])
        gt = sb("gt", [P, T, EXPERTS, EXPERTS])
        eq = sb("eq", [P, T, EXPERTS, EXPERTS])
        rank = sb("rank", [P, T, EXPERTS])
        wsel = sb("wsel", [P, T, EXPERTS])
        gsum = sb("gsum", [P, T])
        grec = sb("grec", [P, T])
        gates = sb("gates", [P, 2, T, EXPERTS])
        gstat = sb("gstat", [P, T, EXPERTS])
        gT = sb("gT", [T * EXPERTS, P])
        al = sb("al", [P, T, MAX_K])
        aeq = sb("aeq", [P, T, MAX_K])
        amax = sb("amax", [P, T])
        kk = sb("kk", [P, T])
        vT, vsq = kbd[0:HID0, 0, :], kbd[0:HID0, 1, :]
        tT, tsq = kbd[0:HID0, 2, :], kbd[0:HID0, 3, :]
        diag = prob[:, 0, :, :]
        den = probT[:, 0, :, :]
        rden = probT[:, 1, :, :]
        norm = sb("norm", [P, 2 * T])
        norm2 = sb("norm2", [P, 2 * T])
        ay, ay2 = ao[0:ACTOR, :, :].rearrange("p t d -> p (t d)"), aoT[0:ACTOR, :]
        ath, aa = qT[0:ACTOR, :], prob[0:ACTOR, 1, :, :].rearrange("p t d -> p (t d)")
        hid = sb("hid", [P, HRING, N])
        tg = sb("tg", [P, 2, N])
        uc = sb("uc", [P, 2, N])
        ytmp = sb("ytmp", [P, 2, T, P])

        up = [bank(f"up{i}") for i in range(BANKS)]
        Y = bank("Y")
        A, B, D = bank("A"), bank("B"), bank("D")
        Y4 = Y[:, :].rearrange("p (t d) -> p t d", t=T)
        A4 = A[:, :].rearrange("p (t d) -> p t d", t=T)
        B4 = B[:, :].rearrange("p (t d) -> p t d", t=T)
        D4 = D[:, :].rearrange("p (t d) -> p t d", t=T)
        heads_out = D[:, 0:HEADS * (HD + 1)].rearrange("p (h d) -> p h d", h=HEADS)

        started = semaphore("started")
        w_loaded = [semaphore(f"w_loaded{L}") for L in range(4)]
        x_loaded = semaphore("x_loaded")
        consts = semaphore("consts")
        alone = semaphore("alone")
        out_done = semaphore("out_done")
        ctx_loaded = semaphore("ctx_loaded")
        gated = [1 if q else 0 for q in GATED]
        proj = signal("proj", [2, 3, 3, 3])
        proj_read = signal("proj_read", [4, 2, 2, 2])
        kv_read = signal("kv_read", [0, 1, 1, 1])
        stats_done = signal("stats_done", 2)
        mom_done = signal("mom_done", 2, 1)
        vare_done = signal("vare_done", 2)
        rstd_done = signal("rstd_done", 2)
        xn_done = signal("xn_done", 2)
        xnT_psum = signal("xnT_psum", 2)
        xnT_done = signal("xnT_done", 2)
        x2T_done = signal("x2T_done", 1)
        cos_psum = signal("cos_psum", [3, 0, 0, 0])
        norm_read = signal("norm_read", [1, 0, 0, 0])
        norm_pool = signal("norm_pool", [2, 0, 0, 0])
        cos_dve = signal("cos_dve", [3, 0, 0, 0])
        score = signal("score", [0, 1, QUADS, QUADS])
        nmax_done = signal("nmax_done", [0, 1, QUADS, QUADS])
        exp_done = signal("exp_done", [0, 1, QUADS, QUADS])
        probT_psum = signal("probT_psum", [0, 1, QUADS, QUADS])
        probT_act = signal("probT_act", [0, 0, QUADS // 2, QUADS // 2])
        probT_dve = signal("probT_dve", [0, 1, QUADS // 2, QUADS // 2])
        av_done = signal("av_done", [0, 1, T, T])
        rsum_done = signal("rsum_done", [0, 1, T, T])
        ao_done = signal("ao_done", [0, 1, T, T], 1)
        aoT_psum = signal("aoT_psum", [0, 0, 1, 1])
        aoT_done = signal("aoT_done", [0, 0, 1, 1])
        wo_done = signal("wo_done", [0, 0, 1, 1])
        bo_done = signal("bo_done", [0, 0, 1, 1])
        resid = signal("resid", 1)
        logits = signal("logits", 1)
        lg_done = signal("lg_done", 1)
        rank_pool = signal("rank_pool", 2)
        compared = signal("compared", 1)
        gstep = signal("gstep", [12, 5, 5, 6])
        dl_done = signal("dl_done", 1)
        ex_done = signal("ex_done", 1)
        gates_done = signal("gates_done", 1)
        act1_psum = signal("act1_psum", [1, 0, 0, 0])
        act1 = signal("act1", [2, 0, 0, 0])
        act_pool = signal("act_pool", [2, 0, 0, 0])
        act_dve = signal("act_dve", [2, 0, 0, 0])
        act2_psum = signal("act2_psum", [1, 0, 0, 0])
        gT_psum = signal("gT_psum", [0, 0, 0, 1])
        gT_done = signal("gT_done", [0, 0, 0, 1])
        b2_psum = signal("b2_psum", [0, 0, 0, 1])
        b2_added = signal("b2_added", [0, 0, 0, 1])
        g_ready = signal("g_ready", CHUNKS)
        u_ready = signal("u_ready", [CHUNKS[L] * gated[L] for L in range(LAYERS)])
        t_ready = signal("t_ready", [CHUNKS[L] * gated[L] for L in range(LAYERS)])
        up_read = [signal(f"up_read{b}", [CHUNKS[L] // (2 if GATED[L] else 4) for L in range(LAYERS)], 1)
                   for b in range(BANKS)]
        hid_ready = signal("hid_ready", [CHUNKS[L] * gated[L] for L in range(LAYERS)], 2)
        y_ready = signal("y_ready", UNITS)
        y_read = signal("y_read", UNITS, 1)
        x_added = signal("x_added", UNITS, 1)

        def up_bank(L, i, which=0):
            return (2 * (i % 2) + which, i // 2) if GATED[L] else (i % 4, i // 4)

        def done_before(L, i):
            n = i - LAG
            return n // PER_UNIT[L] - 1 if n >= PER_UNIT[L] and n % PER_UNIT[L] == 0 else None

        def slots(L, K):
            chunks = CHUNKS[L] if L is not None else 0
            phases = PRE_LEN[K] if K is not None else 0
            n = max(chunks, phases)
            for s in range(n):
                yield ([i for i in range(chunks) if i * n // chunks == s],
                       [p for p in range(phases) if p * n // phases == s])

        LN1, LN2 = 0, 1
        block = ctx.enter_context(nc.Block())

        @block.sync
        def _(sp):
            for s in signals:
                if s.credit:
                    sp.sem_inc(s.sem, s.credit)
            sp.dma_start(x[:, 0, :, :], d["x"][0].rearrange("t p d -> p t d")).then_inc(x_loaded, 16)
            sp.dma_start(const[:, :], d["const"]).then_inc(w_loaded[0], 16)
            sp.dma_start(ctxT[0:C, :], d["ctxT"][0]).then_inc(ctx_loaded, 16)
            small = [(wv0[:, :], "wv0"), (wt0[0:C, :], "wt0"), (wt0[C:C + 1, :], "bt0"), (bv0[:, :], "bv0"),
                     (aw1[:, :], "aw1"), (ab1[:, :], "ab1"), (aw2[:, :], "aw2"),
                     (wr[:, :, :], "wr"), (bq[:, :], "bq"), (wq[:, :, :], "wq"),
                     (wk[0:C, :, :], "wk"), (wk[C:C + 1, :, :], "bk"),
                     (wv[0:C, :, :], "wv"), (wv[C:C + 1, :, :], "bv"), (wo[:, :, :], "wo"),
                     (b1_3[:, :], "b1_3")]
            for dst, name in small:
                sp.dma_start(dst, d[name]).then_inc(w_loaded[0], 16)
            for dst, name in ((ab2[:, :], "ab2"), (bo[:, :, :], "bo"), (br3[:, :], "br3")):
                sp.dma_start(dst, d[name].partition_broadcast(P)).then_inc(w_loaded[0], 16)
            sp.dma_start(wg[0][:, :, :], d["wg0"]).then_inc(w_loaded[0], 16)
            sp.dma_start(wu[0][:, :, :], d["wu0"]).then_inc(w_loaded[0], 16)
            sp.dma_start(wd[0][:, :, :], d["wd0"]).then_inc(w_loaded[0], 16)
            sp.dma_start(x[:, 1:GROUPS, :, :], d["x"][1:GROUPS].rearrange("g t p d -> p g t d")).then_inc(x_loaded, 16)
            sp.wait_ge(consts, 3)
            for t in range(T):
                sp.dma_start(b2_3[EXPERTS * t:EXPERTS * (t + 1), t, :], d["b2_3"]).then_inc(w_loaded[1], 16)
            sp.dma_start(wg[1][:, :, :], d["wg1"]).then_inc(w_loaded[1], 16)
            sp.dma_start(wd[1][:, :, :], d["wd1"]).then_inc(w_loaded[1], 16)
            sp.dma_start(wg[2][:, :, :], d["wg2"]).then_inc(w_loaded[2], 16)
            sp.dma_start(wu[2][:, :, :], d["wu2"]).then_inc(w_loaded[2], 16)
            sp.dma_start(wd[2][:, :, :], d["wd2"]).then_inc(w_loaded[2], 16)

            def load_context(K, g, K0, g0):
                sp.wait_ge(proj.sem, proj.at(K0, g0, proj.per[K0]))
                sp.dma_start(ctxT[0:C, :], d["ctxT"][g]).then_inc(ctx_loaded, 16)

            for L in range(LAYERS):
                with sp.Fori(0, GROUPS - 1) as i:
                    load_context(L, i + 1, L, i)
                    if L == LAYERS - 1:
                        sp.wait_ge(x_added.sem, x_added.at(L, i, UNITS[L]))
                        sp.dma_start(out[i].rearrange("t p d -> p t d"), x[:, i, :, :]).then_inc(out_done, 16)
                if L + 1 < LAYERS:
                    load_context(L + 1, 0, L, GROUPS - 1)
                if L == 0:
                    sp.wait_ge(y_ready.sem, y_ready.at(0, GROUPS - 1, UNITS[0]))
                    sp.dma_start(wg[3], d["wg3"]).then_inc(w_loaded[3], 16)
                    sp.dma_start(wd[3], d["wd3"]).then_inc(w_loaded[3], 16)
            sp.wait_ge(x_added.sem, x_added.at(LAYERS - 1, GROUPS - 1, UNITS[LAYERS - 1]))
            sp.dma_start(out[GROUPS - 1].rearrange("t p d -> p t d"), x[:, GROUPS - 1, :, :]).then_inc(out_done, 16)
            sp.wait_ge(out_done, 16 * GROUPS)

        W0_DMAS = 16 * (1 + 16 + 3 + 3)
        W_TOTAL = [W0_DMAS, 16 * 6, 16 * 3, 16 * 2]

        @block.tensor
        def _(pe):
            pe.wait_ge(w_loaded[0], W_TOTAL[0])
            pe.wait_ge(x_loaded, 32)
            pe.wait_ge(consts, 4)
            pe.wait_ge(started, 2)

            def transpose_norm(K, g, w):
                pe.wait_ge(xn_done.sem, xn_done.at(K, g, w + 1))
                for t in range(T):
                    mm = pe.transpose(D[:, t * P:(t + 1) * P], xn[:, t, :], ident)
                mm.then_inc(xnT_psum.sem, 1)

            def project(K, g, groups_in):
                pe.wait_ge(xnT_done.sem, xnT_done.at(K, g, LN1 + 1))
                if K == 0:
                    pe.matmul(D[0:HID0, :], wv0[:, :], xnT[:, :], start=True, stop=True).then_inc(proj.sem, 1)
                    pe.wait_ge(ctx_loaded, groups_in)
                    pe.sem_inc(alone, 1)
                    pe.matmul(A[0:HID0, :], wt0[:, :], ctxT[:, :], start=True, stop=True).then_inc(proj.sem, 1)
                    return
                pe.matmul(D[:, :], wq[:, K - 1, :], xnT[:, :], start=True, stop=True).then_inc(proj.sem, 1)
                pe.wait_ge(ctx_loaded, groups_in)
                pe.matmul(A[:, :], wk[:, K - 1, :], ctxT[:, :], start=True, stop=True).then_inc(proj.sem, 1)
                for t in range(T):
                    mm = pe.matmul(B4[:, t, :], ctxT[:, t * P:(t + 1) * P], wv[:, K - 1, :], start=True, stop=True)
                mm.then_inc(proj.sem, 1)

            def cosine_products(K, g):
                pe.wait_ge(proj_read.sem, proj_read.at(K, g, 4))
                pe.sem_inc(alone, 1)
                for j, sq in ((0, vsq), (T, tsq)):
                    for t in range(T):
                        mm = pe.matmul(B[:, j + t:j + t + 1], sq[:, t * P:(t + 1) * P], ones[0:HID0, 0:1],
                                       start=True, stop=True)
                mm.then_inc(cos_psum.sem, 1)
                for t in range(T):
                    mm = pe.matmul(A4[:, t, :], vT[:, t * P:(t + 1) * P], tT[:, t * P:(t + 1) * P],
                                   start=True, stop=True)
                mm.then_inc(cos_psum.sem, 1)

            def spread_norms(K, g):
                pe.wait_ge(norm_pool.sem, norm_pool.at(K, g, 2))
                pe.matmul(D[:, :], ones[:, :], diag.rearrange("p t d -> p (t d)"), start=True, stop=True)\
                    .then_inc(cos_psum.sem, 1)

            def scores(K, g, q):
                if K == 1:
                    pe.wait_ge(proj_read.sem, proj_read.at(K, g, 2))
                    for t in range(T):
                        c = slice(t * P, (t + 1) * P)
                        mm = pe.matmul(A4[:, t, :], qT[:, c], kT[:, c], start=True, stop=True)
                    mm.then_inc(score.sem, 1)
                    return
                t, j = q // 4, q % 4
                if q == 0:
                    pe.wait_ge(proj_read.sem, proj_read.at(K, g, 2))
                    pe.wait_ge(kv_read.sem, kv_read.at(K, g, 1))
                else:
                    pe.wait_ge(exp_done.sem, exp_done.at(K, g, q))
                c, r = slice(t * P, (t + 1) * P), slice(32 * j, 32 * j + 32)
                pe.matmul(A4[:, :, :], qT[r, c], kbd[r, :, c], start=True, stop=True).then_inc(score.sem, 1)

            def transpose_probs(K, g, q):
                pe.wait_ge(exp_done.sem, exp_done.at(K, g, q + 1))
                if K > 1 and q == 0:
                    pe.wait_ge(proj_read.sem, proj_read.at(K, g, 2))
                elif K == 1:
                    pe.wait_ge(kv_read.sem, kv_read.at(K, g, 1))
                elif q % 2:
                    pe.wait_ge(probT_dve.sem, probT_dve.at(K, g, (q + 1) // 2))
                else:
                    pe.wait_ge(probT_act.sem, probT_act.at(K, g, q // 2))
                for t in range(T):
                    mm = pe.transpose(B4[:, t, :], prob[:, q % 2, t, :], ident)
                mm.then_inc(probT_psum.sem, 1)

            def weigh_values(K, g, q):
                if K == 1:
                    pe.wait_ge(probT_dve.sem, probT_dve.at(K, g, 1))
                    for t in range(T):
                        mm = pe.matmul(D4[:, t, :], probT[:, 0, t, :], val[:, t, :], start=True, stop=True)
                    mm.then_inc(av_done.sem, 1)
                    return
                t, j = q // 4, q % 4
                if q % 2:
                    pe.wait_ge(probT_act.sem, probT_act.at(K, g, q // 2 + 1))
                else:
                    pe.wait_ge(probT_dve.sem, probT_dve.at(K, g, q // 2 + 1))
                if j == 0 and t:
                    pe.wait_ge(ao_done.sem, ao_done.at(K, g, t))
                for i in range(4):
                    h = 4 * j + i
                    mm = pe.matmul(heads_out[:, h, :], probT[:, q % 2, i, :], va[:, t, h, :], start=True, stop=True)
                if j == 3:
                    mm.then_inc(av_done.sem, 1)

            def transpose_heads(K, g):
                pe.wait_ge(ao_done.sem, ao_done.at(K, g, T))
                for t in range(T):
                    mm = pe.transpose(B4[:, t, :], ao[:, t, :], ident)
                mm.then_inc(aoT_psum.sem, 1)

            def project_out(K, g):
                pe.wait_ge(aoT_done.sem, aoT_done.at(K, g, 1))
                for t in range(T):
                    mm = pe.matmul(A4[:, t, :], aoT[:, t * P:(t + 1) * P], wo[:, K - 2, :], start=True, stop=True)
                mm.then_inc(wo_done.sem, 1)

            def route(K, g):
                pe.wait_ge(xnT_done.sem, xnT_done.at(K, g, LN2 + 1))
                for t in range(T):
                    mm = pe.matmul(B[:, t * EXPERTS:(t + 1) * EXPERTS], xnT[:, t * P:(t + 1) * P], wr[:, K, :],
                                   start=True, stop=True)
                mm.then_inc(logits.sem, 1)

            def pre(K, g, p):
                if p == 1:
                    transpose_norm(K, g, LN1)
                if p == 2:
                    project(K, g, 16 * (g + (GROUPS * K + 1)))
                if K == 0:
                    if p == 3:
                        cosine_products(K, g)
                    if p == 5:
                        spread_norms(K, g)
                elif K == 1:
                    if p == 3:
                        scores(K, g, 0)
                    if p == 4:
                        transpose_probs(K, g, 0)
                    if p == 5:
                        weigh_values(K, g, 0)
                else:
                    if 0 <= p - 3 < QUADS:
                        scores(K, g, p - 3)
                    if 0 <= p - 4 < QUADS:
                        transpose_probs(K, g, p - 4)
                    if 0 <= p - 5 < QUADS:
                        weigh_values(K, g, p - 5)
                    if p == 21:
                        transpose_heads(K, g)
                    if p == 22:
                        project_out(K, g)
                n = NORM2[K]
                if p == n + 1:
                    transpose_norm(K, g, LN2)
                if p == n + 2:
                    route(K, g)
                    if K == 0:
                        pe.matmul(A[0:ACTOR, :], aw1[:, :], xnT[:, :], start=True, stop=True)\
                            .then_inc(act1_psum.sem, 1)
                if K == 0 and p == n + 5:
                    pe.wait_ge(act_dve.sem, act_dve.at(K, g, 2))
                    pe.sem_inc(alone, 1)
                    for t in range(T):
                        mm = pe.matmul(B[:, 64 + t * MAX_K:64 + (t + 1) * MAX_K], aa[:, t * P:(t + 1) * P],
                                       aw2[:, :], start=True, stop=True)
                    mm.then_inc(act2_psum.sem, 1)
                if K == 3 and p == n + 6:
                    pe.wait_ge(gates_done.sem, gates_done.at(K, g, 1))
                    pe.sem_inc(alone, 1)
                    pe.transpose(B[0:T * EXPERTS, 0:P], gstat[:, :, :].rearrange("p t e -> p (t e)"), ident)\
                        .then_inc(gT_psum.sem, 1)
                if K == 3 and p == n + 7:
                    pe.wait_ge(gT_done.sem, gT_done.at(K, g, 1))
                    pe.sem_inc(alone, 1)
                    pe.matmul(A[:, :], gT[:, :], b2_3[:, :, :].rearrange("p t d -> p (t d)"), start=True, stop=True)\
                        .then_inc(b2_psum.sem, 1)

            def up_product(L, g, i):
                rows = ROWS[L]
                if i == 0:
                    pe.wait_ge(x2T_done.sem, x2T_done.at(L, g, 1))
                b, turn = up_bank(L, i)
                pe.wait_ge(up_read[b].sem, up_read[b].at(L, g, turn))
                pe.matmul(up[b][0:rows, :], wg[L][:, i, :], x2T[:, g % 2, :], start=True, stop=True)\
                    .then_inc(g_ready.sem, 1)
                if GATED[L]:
                    b, turn = up_bank(L, i, 1)
                    pe.wait_ge(up_read[b].sem, up_read[b].at(L, g, turn))
                    pe.matmul(up[b][0:rows, :], wu[L][:, i, :], x2T[:, g % 2, :], start=True, stop=True)\
                        .then_inc(u_ready.sem, 1)

            def down_product(L, g, i):
                rows, e, c = ROWS[L], i // PER_UNIT[L], i % PER_UNIT[L]
                if GATED[L]:
                    pe.wait_ge(hid_ready.sem, hid_ready.at(L, g, i + 1))
                else:
                    b, turn = up_bank(L, i)
                    pe.wait_ge(up_read[b].sem, up_read[b].at(L, g, turn + 1))
                if c == 0:
                    pe.wait_ge(y_read.sem, y_read.at(L, g, e))
                for t in range(T):
                    mm = pe.matmul(Y4[:, t, :], hid[0:rows, i % HRING, t * P:(t + 1) * P], wd[L][0:rows, i, :],
                                   start=(c == 0 and t == 0), stop=(c == PER_UNIT[L] - 1), skip_group_check=True)
                if c == PER_UNIT[L] - 1:
                    mm.then_inc(y_ready.sem, 1)

            def trip(L, g, K, gp):
                for chunks, phases in slots(L, K):
                    for i in chunks:
                        up_product(L, g, i)
                        if i >= LAG:
                            down_product(L, g, i - LAG)
                    for p in phases:
                        pre(K, gp, p)
                if L is not None:
                    for i in range(CHUNKS[L] - LAG, CHUNKS[L]):
                        down_product(L, g, i)

            trip(None, None, 0, 0)
            for L in range(LAYERS):
                if L:
                    pe.wait_ge(w_loaded[L], W_TOTAL[L])
                with pe.Fori(0, GROUPS - 1) as i:
                    trip(L, i, L, i + 1)
                trip(L, GROUPS - 1, L + 1 if L + 1 < LAYERS else None, 0)

        @block.scalar
        def _(act):
            act.wait_ge(w_loaded[0], W_TOTAL[0])
            for K in (1, 2, 3):
                scale = float(P) ** -0.5 if K == 1 else float(HD) ** -0.5
                ins = act.activation(bqs[:, K - 1:K], bq[:, K - 1:K], ACT.Copy, scale=scale)
            ins.then_inc(started, 1)
            act.wait_ge(started, 2)

            def evacuate_norm(K, g, w):
                act.wait_ge(xnT_psum.sem, xnT_psum.at(K, g, w + 1))
                act.activation(xnT[:, :], D[:, :], ACT.Copy).then_inc(xnT_done.sem, 1)
                if w == LN2:
                    act.activation(x2T[:, g % 2, :], D[:, :], ACT.Copy).then_inc(x2T_done.sem, 1)

            def read_projections(K, g):
                act.wait_ge(proj.sem, proj.at(K, g, 1))
                if K == 0:
                    act.activation(vT, D[0:HID0, :], ACT.Identity, bias=bv0[:, 0:1]).then_inc(proj_read.sem, 1)
                    act.activation(vsq, D[0:HID0, :], ACT.Square, bias=bv0[:, 0:1]).then_inc(proj_read.sem, 1)
                    act.wait_ge(proj.sem, proj.at(K, g, 2))
                    act.activation(tT, A[0:HID0, :], ACT.Copy).then_inc(proj_read.sem, 1)
                    act.activation(tsq, A[0:HID0, :], ACT.Square).then_inc(proj_read.sem, 1)
                    return
                scale = float(P) ** -0.5 if K == 1 else float(HD) ** -0.5
                act.activation(qT[:, :], D[:, :], ACT.Identity, bias=bqs[:, K - 1:K], scale=scale)\
                    .then_inc(proj_read.sem, 1)
                if K == 1:
                    act.wait_ge(proj.sem, proj.at(K, g, 2))
                    act.activation(kT, A[:, :], ACT.Copy).then_inc(proj_read.sem, 1)
                else:
                    act.wait_ge(proj.sem, proj.at(K, g, 3))
                    act.activation(va[:, :, :, 0:HD].rearrange("p t h d -> p (t h) d"),
                                   B[:, :].rearrange("p (h d) -> p h d", d=HD), ACT.Copy)\
                        .then_inc(proj_read.sem, 1)

            def exponentials(K, g, q):
                act.wait_ge(nmax_done.sem, nmax_done.at(K, g, q + 1))
                for i in range(T):
                    if K == 1:
                        ins = act.activation(prob[:, 0, i, :], A4[:, i, :], ACT.Exp, bias=nmax[:, 0, i:i + 1],
                                             accum_out=sums[:, i:i + 1])
                    else:
                        ins = act.activation(prob[:, q % 2, i, :], A4[:, i, :], ACT.Exp,
                                             bias=nmax[:, q % 2, i:i + 1])
                ins.then_inc(exp_done.sem, 1)

            def evacuate_probs(K, g, q):
                act.wait_ge(probT_psum.sem, probT_psum.at(K, g, q + 1))
                act.activation(probT[:, q % 2, :, :], B4[:, :, :], ACT.Copy).then_inc(probT_act.sem, 1)

            def pre(K, g, p):
                n = NORM2[K]
                if p == 2:
                    evacuate_norm(K, g, LN1)
                if p == 3:
                    read_projections(K, g)
                if K == 1 and p == 4:
                    exponentials(K, g, 0)
                if K > 1:
                    if 0 <= p - 4 < QUADS:
                        exponentials(K, g, p - 4)
                    if 0 <= p - 5 < QUADS and (p - 5) % 2:
                        evacuate_probs(K, g, p - 5)
                    if p == 22:
                        act.wait_ge(aoT_psum.sem, aoT_psum.at(K, g, 1))
                        act.activation(aoT[:, :], B[:, :], ACT.Copy).then_inc(aoT_done.sem, 1)
                if p == n + 2:
                    evacuate_norm(K, g, LN2)
                if p == n + 4:
                    act.wait_ge(dl_done.sem, dl_done.at(K, g, 1))
                    act.activation(ex[:, :, :], dl[:, :, :], ACT.Exp).then_inc(ex_done.sem, 1)
                if K == 0 and p == n + 3:
                    act.wait_ge(act1_psum.sem, act1_psum.at(K, g, 1))
                    act.activation(ay, A[0:ACTOR, :], ACT.Identity, bias=ab1[:, 0:1]).then_inc(act1.sem, 1)
                if K == 0 and p == n + 5:
                    act.wait_ge(act_pool.sem, act_pool.at(K, g, 2))
                    act.activation(ath, ay2, ACT.Tanh, scale=GELU_A).then_inc(act1.sem, 1)
                if K == 3 and p == n + 7:
                    act.wait_ge(gT_psum.sem, gT_psum.at(K, g, 1))
                    act.activation(gT[:, :], B[0:T * EXPERTS, 0:P], ACT.Copy).then_inc(gT_done.sem, 1)

            def hidden(L, g, i):
                rows = ROWS[L]
                if GATED[L]:
                    b, turn = up_bank(L, i)
                    act.wait_ge(g_ready.sem, g_ready.at(L, g, i + 1))
                    act.wait_ge(hid_ready.sem, hid_ready.at(L, g, i - 1))
                    act.activation(tg[0:rows, i % 2, :], up[b][0:rows, :], ACT.Tanh, scale=0.5)\
                        .then_inc(t_ready.sem, 1)
                    b, turn = up_bank(L, i, 1)
                    act.wait_ge(u_ready.sem, u_ready.at(L, g, i + 1))
                    act.activation(uc[0:rows, i % 2, :], up[b][0:rows, :], ACT.Copy).then_inc(up_read[b].sem, 1)
                elif i % 2 == 0:
                    b, turn = up_bank(L, i)
                    act.wait_ge(g_ready.sem, g_ready.at(L, g, i + 1))
                    bias = b1_3[:, i:i + 1] if L == 3 else 0.0
                    act.activation(hid[:, i % HRING, :], up[b][:, :], ACT.Relu, bias=bias)\
                        .then_inc(up_read[b].sem, 1)

            def trip(L, g, K, gp):
                for chunks, phases in slots(L, K):
                    for p in phases:
                        pre(K, gp, p)
                    for i in chunks:
                        hidden(L, g, i)

            trip(None, None, 0, 0)
            for L in range(LAYERS):
                with act.Fori(0, GROUPS - 1) as i:
                    trip(L, i, L, i + 1)
                trip(L, GROUPS - 1, L + 1 if L + 1 < LAYERS else None, 0)

        @block.vector
        def _(dve):
            dve.memset(ctxT[C:C + 1, :], 1.0)
            dve.memset(va[:, :, :, :], 1.0).then_inc(started, 1)
            dve.wait_ge(started, 2)
            dve.wait_ge(w_loaded[0], W_TOTAL[0])
            dve.wait_ge(x_loaded, 32)
            dve.wait_ge(consts, 4)

            def norm_moments(K, g, w):
                if w == LN1 and K > 0:
                    dve.wait_ge(x_added.sem, x_added.at(K - 1, g, UNITS[K - 1]))
                if w == LN2:
                    dve.wait_ge(resid.sem, resid.at(K, g, 1))
                dve.wait_ge(mom_done.sem, mom_done.at(K, g, w))
                dve.sem_inc(alone, 1)
                for t in range(T):
                    ins = dve.bn_stats(stats[:, t, :], x[:, g, t, :])
                ins.then_inc(stats_done.sem, 1)
                dve.wait_ge(stats_done.sem, stats_done.at(K, g, w + 1))
                if True:
                    dve.sem_inc(alone, 1)
                for t in range(T):
                    ins = dve.bn_aggr(moments[:, t, :], stats[:, t, :])
                ins.then_inc(mom_done.sem, 1)

            def normalize(K, g, w):
                dve.wait_ge(rstd_done.sem, rstd_done.at(K, g, w + 1))
                for t in range(T):
                    ins = dve.tensor_scalar(xn[:, t, :], x[:, g, t, :], moments[:, t, 0:1], rstd[:, t:t + 1],
                                            ALU.subtract, ALU.mult)
                ins.then_inc(xn_done.sem, 1)

            def cosine(K, g, p):
                if p == 4:
                    dve.wait_ge(cos_psum.sem, cos_psum.at(K, g, 1))
                    dve.tensor_copy(norm2[:, :], B[:, 0:2 * T]).then_inc(norm_read.sem, 1)
                if p == 6:
                    dve.wait_ge(cos_psum.sem, cos_psum.at(K, g, 3))
                    for t in range(T):
                        ins = dve.tensor_scalar(den[:, t, :], D4[:, t, :], norm[:, t:t + 1], COS_EPS,
                                                ALU.mult, ALU.max)
                    ins.then_inc(cos_dve.sem, 1)
                    dve.wait_ge(cos_dve.sem, cos_dve.at(K, g, 1))
                    dve.reciprocal(rden, den).then_inc(cos_dve.sem, 1)
                    dve.wait_ge(cos_dve.sem, cos_dve.at(K, g, 2))
                    dve.tensor_tensor(tmp[:, :, :], A4[:, :, :], rden, ALU.mult).then_inc(cos_dve.sem, 1)
                    dve.wait_ge(cos_dve.sem, cos_dve.at(K, g, 3))
                    dve.tensor_tensor(x[:, g, :, :], x[:, g, :, :], tmp[:, :, :], ALU.add).then_inc(resid.sem, 1)

            def read_keys_values(K, g):
                if K == 1:
                    dve.wait_ge(proj.sem, proj.at(K, g, 3))
                    dve.tensor_copy(val, B4[:, :, :]).then_inc(kv_read.sem, 1)
                    return
                dve.wait_ge(proj.sem, proj.at(K, g, 2))
                for i in range(4):
                    ins = dve.tensor_scalar(kbd[:, i, :], A[:, :], head_mask[:, i:i + 1], None, ALU.mult)
                ins.then_inc(kv_read.sem, 1)

            def score_max(K, g, q):
                dve.wait_ge(score.sem, score.at(K, g, q + 1))
                dve.tensor_reduce(nmax[:, q % 2, :], A4[:, :, :], AX.X, ALU.max, negate=True)\
                    .then_inc(nmax_done.sem, 1)

            def evacuate_probs(K, g, q):
                dve.wait_ge(probT_psum.sem, probT_psum.at(K, g, q + 1))
                dve.tensor_copy(probT[:, q % 2, :, :], B4[:, :, :]).then_inc(probT_dve.sem, 1)

            def divide_heads(K, g, t):
                dve.wait_ge(av_done.sem, av_done.at(K, g, t + 1))
                dve.reciprocal(rsum[:, :], heads_out[:, :, HD]).then_inc(rsum_done.sem, 1)
                dve.wait_ge(rsum_done.sem, rsum_done.at(K, g, t + 1))
                dve.tensor_tensor(ao[:, t, :].rearrange("p (h d) -> p h d", h=HEADS), heads_out[:, :, 0:HD],
                                  rsum[:, :].unsqueeze(2).to_broadcast([P, HEADS, HD]), ALU.mult)\
                    .then_inc(ao_done.sem, 1)

            def add_attention1(K, g):
                dve.wait_ge(av_done.sem, av_done.at(K, g, 1))
                dve.reciprocal(rsum[:, 0:T], sums[:, :]).then_inc(rsum_done.sem, 1)
                dve.wait_ge(rsum_done.sem, rsum_done.at(K, g, 1))
                dve.tensor_tensor(tmp[:, :, :], D4[:, :, :], rsum[:, 0:T].unsqueeze(2).to_broadcast([P, T, P]),
                                  ALU.mult).then_inc(ao_done.sem, 1)
                dve.wait_ge(ao_done.sem, ao_done.at(K, g, 1))
                dve.tensor_tensor(x[:, g, :, :], x[:, g, :, :], tmp[:, :, :], ALU.add).then_inc(resid.sem, 1)

            def gate_start(K, g):
                dve.wait_ge(logits.sem, logits.at(K, g, 1))
                lgp = B[:, 0:T * EXPERTS].rearrange("p (t e) -> p t e", t=T)
                if K == 3:
                    dve.tensor_tensor(lg[:, :, :], lgp, br3[:, :].unsqueeze(1).to_broadcast([P, T, EXPERTS]),
                                      ALU.add).then_inc(lg_done.sem, 1)
                else:
                    dve.tensor_copy(lg[:, :, :], lgp).then_inc(lg_done.sem, 1)
                dve.wait_ge(lg_done.sem, lg_done.at(K, g, 1))
                full = [P, T, EXPERTS, EXPERTS]
                other = lg[:, :, :].unsqueeze(2).to_broadcast(full)
                own = lg[:, :, :].unsqueeze(3).to_broadcast(full)
                dve.tensor_tensor(gt[:, :, :, :], other, own, ALU.is_gt)
                dve.tensor_tensor(eq[:, :, :, :], other, own, ALU.is_equal).then_inc(compared.sem, 1)
                dve.tensor_reduce(nlmax[:, :], lg[:, :, :], AX.X, ALU.max).then_inc(gstep.sem, 1)
                dve.wait_ge(gstep.sem, gstep.at(K, g, 1))
                dve.tensor_tensor(dl[:, :, :], lg[:, :, :], nlmax[:, :].unsqueeze(2).to_broadcast([P, T, EXPERTS]),
                                  ALU.subtract).then_inc(dl_done.sem, 1)

            def find_k(K, g):
                dve.wait_ge(act2_psum.sem, act2_psum.at(K, g, 1))
                alp = B[:, 64:64 + T * MAX_K].rearrange("p (t k) -> p t k", t=T)
                wide = [P, T, MAX_K]
                dve.scalar_tensor_tensor(out=al[:, :, :], in0=alp, scalar=0.5,
                                         in1=ab2[:, :].unsqueeze(1).to_broadcast(wide),
                                         op0=ALU.mult, op1=ALU.add).then_inc(gstep.sem, 1)
                dve.wait_ge(gstep.sem, gstep.at(K, g, 3))
                dve.tensor_scalar(al[:, :, :], al[:, :, :], 30.0, -30.0, ALU.min, ALU.max).then_inc(gstep.sem, 1)
                dve.wait_ge(gstep.sem, gstep.at(K, g, 4))
                dve.tensor_reduce(amax[:, :], al[:, :, :], AX.X, ALU.max).then_inc(gstep.sem, 1)
                dve.wait_ge(gstep.sem, gstep.at(K, g, 5))
                dve.tensor_tensor(aeq[:, :, :], al[:, :, :], amax[:, :].unsqueeze(2).to_broadcast(wide),
                                  ALU.is_ge).then_inc(gstep.sem, 1)
                dve.wait_ge(gstep.sem, gstep.at(K, g, 6))
                dve.scalar_tensor_tensor(out=al[:, :, :], in0=aeq[:, :, :], scalar=-64.0,
                                         in1=iota1.unsqueeze(1).to_broadcast(wide),
                                         op0=ALU.mult, op1=ALU.add).then_inc(gstep.sem, 1)
                dve.wait_ge(gstep.sem, gstep.at(K, g, 7))
                dve.tensor_reduce(kk[:, :], al[:, :, :], AX.X, ALU.min).then_inc(gstep.sem, 1)
                dve.wait_ge(gstep.sem, gstep.at(K, g, 8))
                dve.scalar_tensor_tensor(out=wsel[:, :, :], in0=rank[:, :, :], scalar=-64.0,
                                         in1=kk[:, :].unsqueeze(2).to_broadcast([P, T, EXPERTS]),
                                         op0=ALU.add, op1=ALU.is_lt).then_inc(gstep.sem, 1)

            def gate_finish(K, g):
                wide = [P, T, EXPERTS]
                k = 9 if K == 0 else 2
                dve.wait_ge(gstep.sem, gstep.at(K, g, k))
                if K == 0:
                    dve.wait_ge(ex_done.sem, ex_done.at(K, g, 1))
                    dve.tensor_tensor(wsel[:, :, :], wsel[:, :, :], ex[:, :, :], ALU.mult).then_inc(gstep.sem, 1)
                else:
                    dve.wait_ge(ex_done.sem, ex_done.at(K, g, 1))
                    dve.scalar_tensor_tensor(out=wsel[:, :, :], in0=rank[:, :, :], scalar=2.0, in1=ex[:, :, :],
                                             op0=ALU.is_lt, op1=ALU.mult).then_inc(gstep.sem, 1)
                dve.wait_ge(gstep.sem, gstep.at(K, g, k + 1))
                dve.tensor_reduce(gsum[:, :], (wsel if K % 2 else ex)[:, :, :], AX.X, ALU.add)\
                    .then_inc(gstep.sem, 1)
                dve.wait_ge(gstep.sem, gstep.at(K, g, k + 2))
                dve.reciprocal(grec[:, :], gsum[:, :]).then_inc(gstep.sem, 1)
                dve.wait_ge(gstep.sem, gstep.at(K, g, k + 3))
                if K == 3:
                    dve.scalar_tensor_tensor(out=gstat[:, :, :], in0=wsel[:, :, :], scalar=GATE_SCALE[K],
                                             in1=grec[:, :].unsqueeze(2).to_broadcast(wide),
                                             op0=ALU.mult, op1=ALU.mult).then_inc(gstep.sem, 1)
                dve.scalar_tensor_tensor(out=gates[:, g % 2, :, :], in0=wsel[:, :, :], scalar=GATE_SCALE[K],
                                         in1=grec[:, :].unsqueeze(2).to_broadcast(wide),
                                         op0=ALU.mult, op1=ALU.mult).then_inc(gates_done.sem, 1)

            def rank_sum(K, g):
                dve.wait_ge(rank_pool.sem, rank_pool.at(K, g, 2))
                dve.tensor_reduce(rank[:, :, :].rearrange("p t e -> p (t e)"),
                                  gt[:, :, :, :].rearrange("p t e j -> p (t e) j"), AX.X, ALU.add)\
                    .then_inc(gstep.sem, 1)

            def pre(K, g, p):
                n = NORM2[K]
                if p == 0:
                    norm_moments(K, g, LN1)
                if p == 1:
                    normalize(K, g, LN1)
                if K == 0:
                    cosine(K, g, p)
                elif K == 1:
                    if p == 3:
                        read_keys_values(K, g)
                        score_max(K, g, 0)
                    if p == 5:
                        evacuate_probs(K, g, 0)
                    if p == 6:
                        add_attention1(K, g)
                else:
                    if p == 3:
                        read_keys_values(K, g)
                    if 0 <= p - 5 < QUADS and (p - 5) % 2 == 0:
                        evacuate_probs(K, g, p - 5)
                    if p >= 9 and (p - 9) % 4 == 0 and (p - 9) // 4 < T - 1:
                        divide_heads(K, g, (p - 9) // 4)
                    if p == 21:
                        divide_heads(K, g, T - 1)
                    if 0 <= p - 3 < QUADS:
                        score_max(K, g, p - 3)
                    if p == 23:
                        dve.wait_ge(wo_done.sem, wo_done.at(K, g, 1))
                        dve.wait_ge(bo_done.sem, bo_done.at(K, g, 1))
                        dve.tensor_tensor(x[:, g, :, :], x[:, g, :, :], A4[:, :, :], ALU.add)\
                            .then_inc(resid.sem, 1)
                if p == n:
                    norm_moments(K, g, LN2)
                if p == n + 1:
                    normalize(K, g, LN2)
                if p == n + 3:
                    gate_start(K, g)
                if p == n + 4:
                    rank_sum(K, g)
                    if K == 0:
                        dve.wait_ge(act_pool.sem, act_pool.at(K, g, 1))
                        dve.tensor_scalar(ay2, ay2, GELU_C, 1.0, ALU.mult, ALU.add).then_inc(act_dve.sem, 1)
                if K == 0 and p == n + 5:
                    dve.wait_ge(act1.sem, act1.at(K, g, 2))
                    dve.scalar_tensor_tensor(out=aa, in0=ath, scalar=1.0, in1=ay, op0=ALU.add, op1=ALU.mult)\
                        .then_inc(act_dve.sem, 1)
                if K == 0 and p == n + 6:
                    find_k(K, g)
                if p == n + (6 if K == 0 else 5):
                    gate_finish(K, g)
                if K == 3 and p == n + 8:
                    dve.wait_ge(b2_psum.sem, b2_psum.at(K, g, 1))
                    dve.tensor_tensor(x[:, g, :, :], x[:, g, :, :], A4[:, :, :], ALU.add).then_inc(b2_added.sem, 1)

            def hidden(L, g, i):
                rows, (b, turn) = ROWS[L], up_bank(L, i)
                if GATED[L]:
                    dve.wait_ge(t_ready.sem, t_ready.at(L, g, i + 1))
                    dve.scalar_tensor_tensor(out=tg[0:rows, i % 2, :], in0=tg[0:rows, i % 2, :], scalar=1.0,
                                             in1=up[b][0:rows, :], op0=ALU.add, op1=ALU.mult)\
                        .then_inc(up_read[b].sem, 1)
                elif i % 2:
                    dve.wait_ge(g_ready.sem, g_ready.at(L, g, i + 1))
                    if L == 3:
                        dve.tensor_scalar(hid[:, i % HRING, :], up[b][:, :], b1_3[:, i:i + 1], 0.0,
                                          ALU.add, ALU.max).then_inc(up_read[b].sem, 1)
                    else:
                        dve.tensor_scalar(hid[:, i % HRING, :], up[b][:, :], 0.0, None, ALU.max)\
                            .then_inc(up_read[b].sem, 1)

            def weigh_expert(L, g, e):
                if e == 0:
                    dve.wait_ge(gates_done.sem, gates_done.at(L, g, 1))
                dve.wait_ge(y_ready.sem, y_ready.at(L, g, e + 1))
                dve.wait_ge(x_added.sem, x_added.at(L, g, max(e - 1, 0)))
                if e == EXPERTS:
                    dve.tensor_scalar(ytmp[:, e % 2, :, :], Y4[:, :, :], SHARED_GATE, None, ALU.mult)\
                        .then_inc(y_read.sem, 1)
                else:
                    dve.tensor_tensor(ytmp[:, e % 2, :, :], Y4[:, :, :],
                                      gates[:, g % 2, :, e].unsqueeze(2).to_broadcast([P, T, P]), ALU.mult)\
                        .then_inc(y_read.sem, 1)

            def trip(L, g, K, gp):
                for chunks, phases in slots(L, K):
                    for i in chunks:
                        if done_before(L, i) is not None:
                            weigh_expert(L, g, done_before(L, i))
                        hidden(L, g, i)
                    for p in phases:
                        pre(K, gp, p)
                if L is not None:
                    for i in range(CHUNKS[L], CHUNKS[L] + LAG):
                        if done_before(L, i) is not None:
                            weigh_expert(L, g, done_before(L, i))
                    weigh_expert(L, g, UNITS[L] - 1)

            trip(None, None, 0, 0)
            for L in range(LAYERS):
                with dve.Fori(0, GROUPS - 1) as i:
                    trip(L, i, L, i + 1)
                trip(L, GROUPS - 1, L + 1 if L + 1 < LAYERS else None, 0)

        @block.gpsimd
        def _(pool):
            pool.memset(ones[:, :], 1.0)
            pool.memset(half[:, 0:8], -0.5)
            pool.memset(half[:, 8:16], 0.5)
            pool.memset(eps[:, :], LN_EPS).then_inc(consts, 1)
            pool.memset(gt[:, :, :, :], 0.0).then_inc(consts, 1)
            pool.memset(b2_3[:, :, :], 0.0).then_inc(consts, 1)
            pool.memset(ytmp[:, :, :, :], 0.0).then_inc(consts, 1)
            pool.wait_ge(consts, 4)
            pool.wait_ge(w_loaded[0], W_TOTAL[0])
            pool.wait_ge(x_loaded, 32)

            def inverse_deviation(K, g, w):
                pool.wait_ge(mom_done.sem, mom_done.at(K, g, w + 1))
                pool.tensor_tensor(vare[:, :], moments[:, :, 1], eps[:, :], ALU.add).then_inc(vare_done.sem, 1)
                pool.wait_ge(vare_done.sem, vare_done.at(K, g, w + 1))
                pool.tensor_tensor(rstd[:, :], vare[:, :], half[:, 0:T], ALU.pow).then_inc(rstd_done.sem, 1)

            def norms(K, g):
                pool.wait_ge(norm_read.sem, norm_read.at(K, g, 1))
                pool.tensor_tensor(norm[:, :], norm2[:, :], half[:, 8:8 + 2 * T], ALU.pow).then_inc(norm_pool.sem, 1)
                pool.wait_ge(norm_pool.sem, norm_pool.at(K, g, 1))
                pool.tensor_tensor(diag, ident.unsqueeze(1).to_broadcast([P, T, P]),
                                   norm[:, T:2 * T].unsqueeze(2).to_broadcast([P, T, P]), ALU.mult)\
                    .then_inc(norm_pool.sem, 1)

            def count_before(K, g):
                full = [P, T, EXPERTS, EXPERTS]
                pool.wait_ge(compared.sem, compared.at(K, g, 1))
                pool.tensor_tensor(eq[:, :, :, :], eq[:, :, :, :], before.unsqueeze(1).to_broadcast(full),
                                   ALU.mult).then_inc(rank_pool.sem, 1)
                pool.wait_ge(rank_pool.sem, rank_pool.at(K, g, 1))
                pool.tensor_tensor(gt[:, :, :, :], gt[:, :, :, :], eq[:, :, :, :], ALU.add)\
                    .then_inc(rank_pool.sem, 1)

            def pre(K, g, p):
                n = NORM2[K]
                if p == 0:
                    inverse_deviation(K, g, LN1)
                if K == 0 and p == 4:
                    norms(K, g)
                if K > 1 and p == 2:
                    pool.wait_ge(xn_done.sem, xn_done.at(K, g, 1))
                    pool.sem_inc(alone, 1)
                    pool.tensor_tensor(x[:, g, :, :], x[:, g, :, :],
                                       bo[:, K - 2, :].unsqueeze(1).to_broadcast([P, T, P]), ALU.add)\
                        .then_inc(bo_done.sem, 1)
                if p == n:
                    inverse_deviation(K, g, LN2)
                if p == n + 3:
                    count_before(K, g)
                if K == 0 and p == n + 4:
                    pool.wait_ge(act1.sem, act1.at(K, g, 1))
                    pool.tensor_tensor(ay2, ay, ay, ALU.mult).then_inc(act_pool.sem, 1)
                    pool.wait_ge(act_dve.sem, act_dve.at(K, g, 1))
                    pool.tensor_tensor(ay2, ay2, ay, ALU.mult).then_inc(act_pool.sem, 1)

            def hidden(L, g, i):
                if GATED[L]:
                    rows = ROWS[L]
                    for which in (0, 1):
                        b, turn = up_bank(L, i, which)
                        pool.wait_ge(up_read[b].sem, up_read[b].at(L, g, turn + 1))
                    pool.tensor_tensor(hid[0:rows, i % HRING, :], tg[0:rows, i % 2, :], uc[0:rows, i % 2, :],
                                       ALU.mult).then_inc(hid_ready.sem, 1)

            def add_expert(L, g, e):
                pool.wait_ge(y_read.sem, y_read.at(L, g, e + 1))
                pool.wait_ge(x_added.sem, x_added.at(L, g, e))
                pool.sem_inc(alone, 1)
                pool.tensor_tensor(x[:, g, :, :], x[:, g, :, :], ytmp[:, e % 2, :, :], ALU.add)\
                    .then_inc(x_added.sem, 1)

            def trip(L, g, K, gp):
                for chunks, phases in slots(L, K):
                    for i in chunks:
                        if done_before(L, i) is not None:
                            add_expert(L, g, done_before(L, i))
                        hidden(L, g, i)
                    for p in phases:
                        pre(K, gp, p)
                if L is not None:
                    for i in range(CHUNKS[L], CHUNKS[L] + LAG):
                        if done_before(L, i) is not None:
                            add_expert(L, g, done_before(L, i))
                    add_expert(L, g, UNITS[L] - 1)

            trip(None, None, 0, 0)
            for L in range(LAYERS):
                with pool.Fori(0, GROUPS - 1) as i:
                    trip(L, i, L, i + 1)
                trip(L, GROUPS - 1, L + 1 if L + 1 < LAYERS else None, 0)


def kernel(**inputs):
    import numpy as np
    import concourse.bacc as bacc
    from concourse.bass_utils import run_bass_kernel_spmd

    a = {k: np.asarray(v) for k, v in inputs.items()}
    ident = np.eye(P, dtype=np.float32)
    head_mask = (np.arange(P)[:, None] // HD % 4 == np.arange(4)[None, :]).astype(np.float32)
    before = np.broadcast_to(np.tril(np.ones((EXPERTS, EXPERTS), np.float32), -1).reshape(1, 64), (P, 64))
    iota1 = np.broadcast_to(np.arange(1, MAX_K + 1, dtype=np.float32)[None, :], (P, MAX_K))
    e, r0 = EXPERTS, ROWS[0]

    def columns(w):
        return w.transpose(1, 0, 2).reshape(P, -1, P)

    def rows(w):
        return w.reshape(-1, P, P).transpose(1, 0, 2)

    host = {
        "const": np.concatenate([ident, head_mask, before, iota1], axis=1),
        "x": a["x"].reshape(GROUPS, T, P, P),
        "ctxT": a["ctx_768"].reshape(GROUPS, N, C).transpose(0, 2, 1),
        "wv0": a["L0_xattn_Wv"].T, "wt0": a["L0_xattn_Wt"].T,
        "bt0": a["L0_xattn_bt"].reshape(1, HID0), "bv0": a["L0_xattn_bv"].reshape(HID0, 1),
        "aw1": a["L0_ffn_actor_w1"].T, "ab1": a["L0_ffn_actor_b1"].reshape(ACTOR, 1),
        "aw2": a["L0_ffn_actor_w2"].T, "ab2": a["L0_ffn_actor_b2"],
        "wr": np.stack([a["L0_ffn_router_w"].T, a["L1_ffn_Wr"], a["L2_ffn_gate_W"].T, a["L3_ffn_Wr"]], axis=1),
        "br3": a["L3_ffn_br"],
        "bq": np.stack([a[f"L{K}_xattn_bq"] for K in (1, 2, 3)], axis=1),
        "wq": np.stack([a["L1_xattn_Wq"], a["L2_xattn_Wq"], a["L3_xattn_Wq"].T], axis=1),
        "wk": np.stack([a["L1_xattn_Wk"], a["L2_xattn_Wk"], a["L3_xattn_Wk"].T], axis=1),
        "wv": np.stack([a["L1_xattn_Wv"], a["L2_xattn_Wv"], a["L3_xattn_Wv"].T], axis=1),
        "bk": np.stack([a[f"L{K}_xattn_bk"] for K in (1, 2, 3)])[None],
        "bv": np.stack([a[f"L{K}_xattn_bv"] for K in (1, 2, 3)])[None],
        "wo": np.stack([a["L2_xattn_Wo"], a["L3_xattn_Wo"].T], axis=1),
        "bo": np.stack([a["L2_xattn_bo"], a["L3_xattn_bo"]]),
        "wg0": a["L0_ffn_gate_w"].reshape(-1, r0, P).transpose(2, 0, 1),
        "wu0": a["L0_ffn_up_w"].reshape(-1, r0, P).transpose(2, 0, 1),
        "wd0": a["L0_ffn_down_w"].reshape(e, P, PER_UNIT[0], r0).transpose(3, 0, 2, 1).reshape(r0, -1, P),
        "wg1": columns(a["L1_ffn_W1"]), "wd1": rows(a["L1_ffn_W2"]),
        "wg2": np.concatenate([columns(a["L2_ffn_w1_e"]), columns(a["L2_ffn_w1_s"])], axis=1),
        "wu2": np.concatenate([columns(a["L2_ffn_w3_e"]), columns(a["L2_ffn_w3_s"])], axis=1),
        "wd2": np.concatenate([rows(a["L2_ffn_w2_e"]), rows(a["L2_ffn_w2_s"])], axis=1),
        "wg3": columns(a["L3_ffn_W1"]), "wd3": rows(a["L3_ffn_W2"]),
        "b1_3": a["L3_ffn_b1"].reshape(-1, P).T, "b2_3": a["L3_ffn_b2"],
    }
    nc = bacc.Bacc("TRN2", target_bir_lowering=False, num_devices=1)
    arrays, dram = {}, {}
    for name, v in host.items():
        arrays[f"in_{name}"] = np.ascontiguousarray(v)
        dram[name] = nc.dram_tensor(f"in_{name}", v.shape, F32, kind="ExternalInput").ap()
    out = nc.dram_tensor("out_0", (GROUPS, T, P, P), F32, kind="ExternalOutput").ap()
    build(nc, dram, out)
    r = run_bass_kernel_spmd(nc, [arrays], core_ids=[0])
    return r.results[0]["out_0"].reshape(GROUPS * T, P, P)
```

```python
from contextlib import ExitStack

import concourse.bass as bass
from concourse import mybir

ALU = mybir.AluOpType
ACT = mybir.ActivationFunctionType
AX = mybir.AxisListType
F32 = mybir.dt.float32
U32 = mybir.dt.uint32

P = 128
GROUPS = 8
T = 4
N = T * P
C = 96
EXPERTS = 8
LAYERS = 4
HEADS, HD = 16, 8
QUADS = T * 4
HID0 = 64
ACTOR, MAX_K = 50, 6
LN_EPS, COS_EPS = 1e-5, 1e-8
GELU_A, GELU_C = 0.7978845608028654, 0.044715

ROWS = [112, 128, 128, 128]
PER_UNIT = [3, 4, 4, 2]
UNITS = [8, 8, 9, 8]
GATED = [True, False, True, False]
CHUNKS = [a * b for a, b in zip(PER_UNIT, UNITS)]
LAG = 2
HRING = 4
BANKS = 4

NORM2 = [7, 7, 24, 24, None]
PRE_LEN = [NORM2[0] + 8, NORM2[1] + 9, NORM2[2] + 9, NORM2[3] + 9, 1]
GATE_SCALE = [0.5, 1.0, 0.25, 1.0]
SHARED_GATE = 0.5 * 0.5 / 8


STEPS = GROUPS // 2
BLOCKS = [(1, 0, None), (1, 4, 1), (2, 0, 1), (2, 4, 2), (3, 0, 2), (3, 4, 3), (4, 0, 3), (4, 4, None)]
MAX_TILES = 40
QUOTA = MAX_TILES // STEPS
SHARED = T
TILES = [(QUOTA if L is not None else 0) + (SHARED if K == 2 else 0) for K, _, L in BLOCKS]
LIST = STEPS * N
ROWS_D = EXPERTS * LIST + MAX_TILES * P
RING = 4
HIDDEN = {1: 512, 2: 512, 3: 256}
TURNS = {2: [0, 1, 2, 4, 5, 6, 7, 8, 9, 10, 11, 27, 28, 29, 30, 31, 32, 33],
         3: [0, 1, 2, 5, 6, 7, 8, 9, 10, 11, 12, 13, 14, 15]}
CLEARED = ROWS_D // P // T // (GROUPS - 1)
DEPTH = 4


class Signal:

    def __init__(self, sem, per, credit=0, units=LAYERS + 1, reps=GROUPS):
        self.sem, self.credit = sem, credit
        self.per = [per] * units if isinstance(per, int) else list(per) + [0] * (units - len(per))
        self.base = [reps * sum(self.per[:L]) for L in range(units)]

    def at(self, layer, g, k):
        return g * self.per[layer] + (self.base[layer] + self.credit + k)


def build(nc, d, out):
    with ExitStack() as ctx:
        def sb(name, shape):
            return ctx.enter_context(nc.sbuf_tensor(name, shape, F32))

        def bank(name):
            return ctx.enter_context(nc.psum_tensor(name, [P, N], F32))

        def semaphore(name):
            return ctx.enter_context(nc.semaphore(name))

        signals = []

        def signal(name, per, credit=0, **counted):
            s = Signal(semaphore(name), per, credit, **counted)
            signals.append(s)
            return s

        x = sb("x", [P, GROUPS, T, P])
        const = sb("const", [P, 2 * P + 4 + 64 + MAX_K + 8 + 16 + MAX_TILES])
        ident = const[:, 0:P]
        head_mask = const[:, P:P + 4]
        before = const[:, P + 4:P + 68].rearrange("p (e j) -> p e j", j=EXPERTS)
        iota1 = const[:, P + 68:P + 68 + MAX_K]
        tail = const[:, P + 68 + MAX_K:]
        earlier = tail[:, 0:P]
        list_start = tail[:, P:P + 8]
        tile_start = tail[:, P + 8:P + 24]
        iota_tile = tail[:, P + 24:P + 24 + MAX_TILES]
        ones = sb("ones", [P, P])
        half = sb("half", [P, 16])
        eps = sb("eps", [P, T])
        wg = {0: sb("wg0", [P, CHUNKS[0], ROWS[0]]), 1: sb("w1_1", [P, CHUNKS[1], P]),
              2: sb("wg2", [P, CHUNKS[2], P])}
        wu = {0: sb("wu0", [P, CHUNKS[0], ROWS[0]]), 2: sb("wu2", [P, CHUNKS[2], P])}
        wd = {0: sb("wd0", [ROWS[0], CHUNKS[0], P]), 1: sb("wd1", [P, CHUNKS[1], P]),
              2: sb("wd2", [P, CHUNKS[2], P])}
        wg[3] = wg[0][:, :, :].rearrange("p c r -> p (c r)")[:, 0:CHUNKS[3] * P] \
            .rearrange("p (c r) -> p c r", r=P)
        wd[3] = wu[0][:, :, :].rearrange("p c r -> p (c r)")[:, 0:CHUNKS[3] * P] \
            .rearrange("p (c r) -> p c r", r=P)
        biases = wg[1][:, 0:CHUNKS[3] + EXPERTS, :].rearrange("p c r -> p (c r)")
        b1_3, b2_3 = biases[:, 0:CHUNKS[3] * P], biases[:, CHUNKS[3] * P:]
        wv0 = sb("wv0", [P, HID0])
        wt0 = sb("wt0", [C + 1, HID0])
        wq = sb("wq", [P, 3, P])
        wk = sb("wk", [C + 1, 3, P])
        wv = sb("wv", [C + 1, 3, P])
        wo = sb("wo", [P, 2, P])
        bo = sb("bo", [P, 2, P])
        bv0 = sb("bv0", [HID0, 1])
        bq = sb("bq", [P, 3])
        bqs = sb("bqs", [P, 3])
        wr = sb("wr", [P, 4, EXPERTS])
        br3 = sb("br3", [P, EXPERTS])
        aw1 = sb("aw1", [P, ACTOR])
        ab1 = sb("ab1", [ACTOR, 1])
        aw2 = sb("aw2", [ACTOR, MAX_K])
        ab2 = sb("ab2", [P, MAX_K])
        ctxT = sb("ctxT", [C + 1, N])
        stats = sb("stats", [P, T, 6])
        moments = sb("moments", [P, T, 2])
        vare = sb("vare", [P, T])
        rstd = sb("rstd", [P, T])
        xn = sb("xn", [P, T, P])
        xnT = sb("xnT", [P, N])
        x2T = sb("x2T", [P, 2, N])
        qT = sb("qT", [P, N])
        kbd = sb("kbd", [P, T, N])
        kT = kbd[:, 0, :]
        va = sb("va", [P, T, P])
        val = kbd[:, 1, :].rearrange("p (t d) -> p t d", t=T)
        nmax = sb("nmax", [P, 2, T])
        prob = sb("prob", [P, 2, T, P])
        probT = sb("probT", [P, 2, T, P])
        sums = sb("sums", [P, 2, T])
        rsum = sb("rsum", [P, HEADS])
        ao = sb("ao", [P, T, P])
        aoT = sb("aoT", [P, N])
        tmp = ao
        lg = sb("lg", [P, T, EXPERTS])
        nlmax = sb("nlmax", [P, T])
        dl = sb("dl", [P, T, EXPERTS])
        ex = sb("ex", [P, T, EXPERTS])
        gt = sb("gt", [P, T, EXPERTS, EXPERTS])
        eq = sb("eq", [P, T, EXPERTS, EXPERTS])
        rank = sb("rank", [P, T, EXPERTS])
        wsel = sb("wsel", [P, T, EXPERTS])
        gsum = sb("gsum", [P, T])
        grec = sb("grec", [P, T])
        gates = sb("gates", [P, 2, T, EXPERTS])
        gstat = sb("gstat", [P, T, EXPERTS])
        al = sb("al", [P, T, MAX_K])
        aeq = sb("aeq", [P, T, MAX_K])
        amax = sb("amax", [P, T])
        kk = sb("kk", [P, T])
        vT, vsq = kbd[0:HID0, 0, :], kbd[0:HID0, 1, :]
        tT, tsq = kbd[0:HID0, 2, :], kbd[0:HID0, 3, :]
        diag = prob[:, 0, :, :]
        den = probT[:, 0, :, :]
        rden = probT[:, 1, :, :]
        norm = sb("norm", [P, 2 * T])
        norm2 = sb("norm2", [P, 2 * T])
        ay, ay2 = ao[0:ACTOR, :, :].rearrange("p t d -> p (t d)"), aoT[0:ACTOR, :]
        ath, aa = qT[0:ACTOR, :], prob[0:ACTOR, 1, :, :].rearrange("p t d -> p (t d)")
        xn2 = sb("xn2", [P, T, P])
        mask = sb("mask", [P, T, EXPERTS])
        next_row = sb("next_row", [P, EXPERTS])
        place = sb("place", [P, T, EXPERTS])
        pick = sb("pick", [P, 4, T, EXPERTS])
        picked = sb("picked", [P, 4, T])
        routes = sb("routes", [P, GROUPS, 4, T])
        pos_now = ctx.enter_context(nc.sbuf_tensor("pos_now", [P, 2, T], U32))
        pos_back = ctx.enter_context(nc.sbuf_tensor("pos_back", [P, 2, T], U32))
        gate_back = sb("gate_back", [P, 2, T])
        filled = sb("filled", [P, EXPERTS])
        ntile = sb("ntile", [P, EXPERTS])
        tprev = sb("tprev", [P, EXPERTS])
        tend = sb("tend", [P, EXPERTS])
        flat_gt = gt[:, :, :, :].rearrange("p t e j -> p (t e j)")
        tcmp = flat_gt[:, 0:16 * EXPERTS].rearrange("p (e k) -> p e k", e=EXPERTS)
        ncmp = flat_gt[:, 16 * EXPERTS:24 * EXPERTS].rearrange("p (e k) -> p e k", e=EXPERTS)
        jcmp = aoT[:, 0:MAX_TILES * EXPERTS].rearrange("p (j e) -> p j e", e=EXPERTS)
        jcmp2 = ao[:, :, :].rearrange("p t d -> p (t d)")[:, 0:MAX_TILES * EXPERTS] \
            .rearrange("p (j e) -> p j e", e=EXPERTS)
        flat_eq = eq[:, :, :, :].rearrange("p t e j -> p (t e j)")
        tile_e, tile_o, tile_k, tile_r = (flat_eq[:, k * MAX_TILES:(k + 1) * MAX_TILES] for k in range(4))
        table = ctx.enter_context(nc.sbuf_tensor("table", [P, 2, 2, MAX_TILES], U32))
        zeros = xn2[:, :, :].rearrange("p t d -> p (t d)")
        hid = sb("hid", [P, HRING, N])
        tg = sb("tg", [P, 2, N])
        uc = sb("uc", [P, 2, N])
        ytmp = sb("ytmp", [P, 2, T, P])
        xs, ys = (uc[:, k, :].rearrange("p (r d) -> p r d", r=RING) for k in range(2))
        xsT = x2T[:, 1, 0:2 * P].rearrange("p (k d) -> p k d", k=2)
        yg = ytmp

        hs, hsT = hid[:, 0:2, :], hid[:, 2:4, :]

        lists = [nc.dram_tensor(f"list{k}", (ROWS_D, P), F32).ap() for k in range(3)]

        up = [bank(f"up{i}") for i in range(BANKS)]
        Y = bank("Y")
        A, B, D = bank("A"), bank("B"), bank("D")
        Y4 = Y[:, :].rearrange("p (t d) -> p t d", t=T)
        A4 = A[:, :].rearrange("p (t d) -> p t d", t=T)
        B4 = B[:, :].rearrange("p (t d) -> p t d", t=T)
        D4 = D[:, :].rearrange("p (t d) -> p t d", t=T)
        G, U, TH = up[0:3]
        scores_in = [A4, up[3][:, :].rearrange("p (t d) -> p t d", t=T)]
        YT = Y[:, 0:P]
        XT = Y[:, P:2 * P]

        started = semaphore("started")
        w_loaded = [semaphore(f"w_loaded{L}") for L in range(4)]
        x_loaded = semaphore("x_loaded")
        rest_loaded = semaphore("rest_loaded")
        consts = semaphore("consts")
        alone = semaphore("alone")
        out_done = semaphore("out_done")
        ctx_loaded = semaphore("ctx_loaded")
        gated = [1 if q else 0 for q in GATED]
        proj = signal("proj", [2, 3, 3, 3])
        proj_read = signal("proj_read", [4, 2, 2, 2])
        kv_read = signal("kv_read", [0, 1, 1, 1])
        stats_done = signal("stats_done", 2)
        mom_done = signal("mom_done", 2, 1)
        vare_done = signal("vare_done", 2)
        rstd_done = signal("rstd_done", 2)
        xn_done = signal("xn_done", 2)
        xnT_psum = signal("xnT_psum", 2)
        xnT_done = signal("xnT_done", 2)
        x2T_done = signal("x2T_done", [1, 0, 1, 0])
        cos_psum = signal("cos_psum", [3, 0, 0, 0])
        norm_read = signal("norm_read", [1, 0, 0, 0])
        norm_pool = signal("norm_pool", [2, 0, 0, 0])
        cos_dve = signal("cos_dve", [3, 0, 0, 0])
        score = signal("score", [0, 1, QUADS, QUADS])
        nmax_done = signal("nmax_done", [0, 1, QUADS, QUADS])
        exp_done = signal("exp_done", [0, 1, QUADS, QUADS])
        probT_psum = signal("probT_psum", [0, 1, QUADS, QUADS])
        probT_act = signal("probT_act", [0, 0, QUADS // 2, QUADS // 2])
        probT_dve = signal("probT_dve", [0, 1, QUADS // 2, QUADS // 2])
        av_done = signal("av_done", [0, 1, T, T])
        rsum_done = signal("rsum_done", [0, 1, QUADS, QUADS])
        prob_done = signal("prob_done", [0, 0, QUADS, QUADS])
        ao_done = signal("ao_done", [0, 1, T, T], 1)
        aoT_done = signal("aoT_done", [0, 0, T, T])
        wo_done = signal("wo_done", [0, 0, 1, 1])
        bo_done = signal("bo_done", [0, 0, 1, 1])
        resid = signal("resid", 1)
        logits = signal("logits", 1)
        lg_done = signal("lg_done", 1)
        rank_pool = signal("rank_pool", 2)
        compared = signal("compared", 1)
        gstep = signal("gstep", [12, 5, 5, 5])
        dl_done = signal("dl_done", 1)
        ex_done = signal("ex_done", 1)
        gates_done = signal("gates_done", 1)
        act1_psum = signal("act1_psum", [1, 0, 0, 0])
        act1 = signal("act1", [2, 0, 0, 0])
        act_pool = signal("act_pool", [2, 0, 0, 0])
        act_dve = signal("act_dve", [2, 0, 0, 0])
        act2_psum = signal("act2_psum", [1, 0, 0, 0])
        g_ready = signal("g_ready", [CHUNKS[0]])
        u_ready = signal("u_ready", [CHUNKS[0]])
        t_ready = signal("t_ready", [CHUNKS[0]])
        up_read = [signal(f"up_read{b}", [CHUNKS[0] // 2], 1) for b in range(BANKS)]
        hid_ready = signal("hid_ready", [CHUNKS[0]], 2)
        y_ready = signal("y_ready", [EXPERTS])
        y_read = signal("y_read", [EXPERTS], 1)
        x_added = signal("x_added", [EXPERTS], 1)
        mask_done = signal("mask_done", [0, 1, 1, 1])
        place_psum = signal("place_psum", [0, 1, 1, 1])
        rstep = signal("rstep", [0, 4, 4, 4])
        pos_done = signal("pos_done", [0, 1, 1, 1])
        scattered = signal("scattered", [0, 16 * 2 * T, 16 * 2 * T, 16 * 2 * T])
        recalled = signal("recalled", [0, 0, 1, 1, 1])
        gathered = [signal(f"gathered{s}", [0, 0, 16 * T, 16 * T, 16 * T]) for s in range(2)]
        cstep = signal("cstep", [0, 0, 1, 1, 1])
        combined = signal("combined", [0, 0, 1, 1, 1], 1)
        zeroed = semaphore("zeroed")

        def tile_signal(name, per, credit=0):
            return signal(name, per, credit, units=len(BLOCKS), reps=STEPS)

        routed = [0 if L is None else QUOTA for _, _, L in BLOCKS]
        pairs = [TILES[b] if BLOCKS[b][2] == 2 else TILES[b] - routed[b] for b in range(len(BLOCKS))]

        def by_slot(name, credit=0):
            return [tile_signal(f"{name}{r}", [16 * len(range(r, n, RING)) for n in routed], credit)
                    for r in range(RING)]

        tstep = signal("tstep", [11 * (n > 0) for n in routed], units=len(BLOCKS), reps=1)
        table_done = signal("table_done", [int(n > 0) for n in routed], units=len(BLOCKS), reps=1)
        xs_loaded = by_slot("xs_loaded")
        xsT_psum = tile_signal("xsT_psum", routed, 1)
        xsT_done = tile_signal("xsT_done", routed)
        tile_g = tile_signal("tile_g", TILES)
        tile_u = tile_signal("tile_u", pairs)
        tile_t = tile_signal("tile_t", pairs)
        tile_b = tile_signal("tile_b", [n * (BLOCKS[b][2] == 3) for b, n in enumerate(routed)])
        tile_w = tile_signal("tile_w", pairs)
        tile_h = tile_signal("tile_h", TILES, 1)
        hT_psum = tile_signal("hT_psum", TILES)
        hT_done = tile_signal("hT_done", TILES)
        tile_y = tile_signal("tile_y", TILES)
        tile_y_read = tile_signal("tile_y_read", TILES, 1)
        y_stored = by_slot("y_stored", 1)

        def up_bank(L, i, which=0):
            return 2 * (i % 2) + which, i // 2

        def done_before(L, i):
            n = i - LAG
            return n // PER_UNIT[L] - 1 if n >= PER_UNIT[L] and n % PER_UNIT[L] == 0 else None

        def slots(L, K):
            chunks = CHUNKS[L] if L is not None else 0
            phases = PRE_LEN[K] if K is not None else 0
            n = max(chunks, phases)
            for s in range(n):
                yield ([i for i in range(chunks) if i * n // chunks == s],
                       [p for p in range(phases) if p * n // phases == s])

        def first_group(eng, pre):
            for p in range(PRE_LEN[0]):
                pre(0, 0, p)
            eng.wait_ge(rest_loaded, 4 * 16)

        def step_slots(b):
            K = BLOCKS[b][0]
            phases = PRE_LEN[K]
            turns = TILES[b] + DEPTH if TILES[b] else 0
            if K in (2, 3):
                at = TURNS[K]
            else:
                at = [n * max(phases, turns) // turns for n in range(turns)]
            for s in range(max([phases] + [a + 1 for a in at])):
                yield ([n for n in range(turns) if at[n] == s],
                       [p for p in range(phases) if p * (1 if K == 2 else max(phases, turns)) //
                        (1 if K == 2 else phases) == s])

        def staged(b, n):
            return [n - a if 0 <= n - a < TILES[b] else None for a in (0, 1, 3, DEPTH)]

        def tile_layer(b, j):
            shared = j >= routed[b]
            return (2 if shared else BLOCKS[b][2]), shared

        def up_of(b, j):
            return G if tile_layer(b, j)[0] == 2 or j % 2 == 0 else U

        def pair(b, j):
            return j if BLOCKS[b][2] == 2 else j - routed[b]

        def run(first, trip, before_block, step, eng):
            first()
            with eng.Fori(0, GROUPS - 1) as i:
                trip(i, 0, i + 1)
            trip(GROUPS - 1, 1, 0)
            for b, (K, g0, L) in enumerate(BLOCKS):
                if b:
                    before_block(b, K, g0, L)
                with eng.Fori(1 if b == 0 else 0, STEPS - 1) as i:
                    step(b, i, K, i + g0, False)
                step(b, STEPS - 1, K, STEPS - 1 + g0, True)

        LN1, LN2 = 0, 1
        block = ctx.enter_context(nc.Block())

        @block.sync
        def _(sp):
            for s in signals:
                if s.credit:
                    sp.sem_inc(s.sem, s.credit)
            sp.dma_start(x[:, 0, :, :], d["x"][0].rearrange("t p d -> p t d")).then_inc(x_loaded, 16)
            sp.dma_start(const[:, :], d["const"]).then_inc(w_loaded[0], 16)
            sp.dma_start(ctxT[0:C, :], d["ctxT"][0]).then_inc(ctx_loaded, 16)
            small = [(wv0[:, :], "wv0"), (wt0[0:C, :], "wt0"), (wt0[C:C + 1, :], "bt0"), (bv0[:, :], "bv0"),
                     (aw1[:, :], "aw1"), (ab1[:, :], "ab1"), (aw2[:, :], "aw2"),
                     (wr[:, :, :], "wr"), (bq[:, :], "bq"), (wq[:, :, :], "wq"),
                     (wk[0:C, :, :], "wk"), (wk[C:C + 1, :, :], "bk"),
                     (wv[0:C, :, :], "wv"), (wv[C:C + 1, :, :], "bv"), (wo[:, :, :], "wo")]
            for dst, name in small:
                sp.dma_start(dst, d[name]).then_inc(w_loaded[0], 16)
            for dst, name in ((ab2[:, :], "ab2"), (bo[:, :, :], "bo"), (br3[:, :], "br3")):
                sp.dma_start(dst, d[name].partition_broadcast(P)).then_inc(w_loaded[0], 16)
            sp.dma_start(wg[0][:, :, :], d["wg0"]).then_inc(rest_loaded, 16)
            sp.dma_start(wu[0][:, :, :], d["wu0"]).then_inc(rest_loaded, 16)
            sp.dma_start(wd[0][:, :, :], d["wd0"]).then_inc(rest_loaded, 16)
            sp.dma_start(x[:, 1:GROUPS, :, :], d["x"][1:GROUPS].rearrange("g t p d -> p g t d")).then_inc(rest_loaded, 16)

            sp.wait_ge(consts, 4)

            def load_context(g, K0, g0):
                sp.wait_ge(proj.sem, proj.at(K0, g0, proj.per[K0]))
                sp.dma_start(ctxT[0:C, :], d["ctxT"][g]).then_inc(ctx_loaded, 16)

            def trip(g, K, gp):
                if K == 0:
                    load_context(gp, 0, g)
                    for rows in lists:
                        sp.dma_start(rows.rearrange("(p r a) d -> p r (a d)", p=P, a=T)[:, bass.ds(g * CLEARED, CLEARED), :],
                                     zeros.unsqueeze(1).to_broadcast([P, CLEARED, N])).then_inc(zeroed, 16)
                    return
                load_context(0, 0, GROUPS - 1)
                sp.dma_start(wg[1][:, :, :], d["wg1"]).then_inc(w_loaded[1], 16)
                sp.dma_start(wd[1][:, :, :], d["wd1"]).then_inc(w_loaded[1], 16)
                sp.dma_start(wg[2][:, :, :], d["wg2"]).then_inc(w_loaded[2], 16)
                sp.dma_start(wu[2][:, :, :], d["wu2"]).then_inc(w_loaded[2], 16)
                sp.dma_start(wd[2][:, :, :], d["wd2"]).then_inc(w_loaded[2], 16)
                load_context(1, 1, 0)
                sp.wait_ge(y_ready.sem, y_ready.at(0, GROUPS - 1, EXPERTS))
                sp.dma_start(wg[3], d["wg3"]).then_inc(w_loaded[3], 16)
                sp.dma_start(wd[3], d["wd3"]).then_inc(w_loaded[3], 16)

            def before_block(b, K, g0, L):
                if b == 3:
                    sp.wait_ge(tile_y.sem, tile_y.at(2, STEPS - 1, TILES[2]))
                    sp.dma_start(b1_3, d["b1_3"].partition_broadcast(P)).then_inc(w_loaded[3], 16)
                    sp.dma_start(b2_3, d["b2_3"].partition_broadcast(P)).then_inc(w_loaded[3], 16)
                if L is not None:
                    sp.wait_ge(scattered.sem, scattered.at(BLOCKS[b - 1][0], BLOCKS[b - 1][1] + STEPS - 1, 32 * T))
                    sp.wait_ge(table_done.sem, table_done.at(b, 0, 1))

            def tile_row(b, i, j):
                return sp.value_load(table[0:1, b % 2, 1, bass.ds(i * QUOTA + j, 1)],
                                     min_val=0, max_val=ROWS_D - P)

            def load_tile(b, i, j):
                row = tile_row(b, i, j)
                if j == 0 or j >= RING:
                    sp.wait_ge(xsT_psum.sem, xsT_psum.at(b, i, max(j - RING + 1, 0)))
                sp.dma_start(xs[:, j % RING, :], lists[(b - 1) % 3][bass.ds(row, P), :])\
                    .then_inc(xs_loaded[j % RING].sem, 16)

            def store_tile(b, i, j):
                row = tile_row(b, i, j)
                sp.wait_ge(tile_y_read.sem, tile_y_read.at(b, i, j + 1))
                sp.dma_start(lists[(b - 1) % 3][bass.ds(row, P), :], ys[:, j % RING, :])\
                    .then_inc(y_stored[j % RING].sem, 16)

            def load_next(b, K, g, last):
                if K == 4:
                    sp.wait_ge(combined.sem, combined.at(K, g, 1))
                    sp.dma_start(out[g].rearrange("t p d -> p t d"), x[:, g, :, :]).then_inc(out_done, 16)
                elif not last:
                    load_context(g + 1, K, g)
                elif BLOCKS[b + 1][0] < 4:
                    load_context(BLOCKS[b + 1][1], K, g)

            def step(b, i, K, g, last):
                behind = RING + DEPTH
                for j in range(routed[b]):
                    load_tile(b, i, j)
                    if j == RING - 1:
                        load_next(b, K, g, last)
                    if j >= behind:
                        store_tile(b, i, j - behind)
                for j in range(max(routed[b] - behind, 0), routed[b]):
                    store_tile(b, i, j)
                if not routed[b]:
                    load_next(b, K, g, last)

            run(lambda: None, trip, before_block, step, sp)
            sp.wait_ge(out_done, 16 * GROUPS)

        W0_DMAS = 16 * (1 + 15 + 3)
        W_TOTAL = [W0_DMAS, 16 * 2, 16 * 3, 16 * 4]

        @block.tensor
        def _(pe):
            pe.wait_ge(w_loaded[0], W_TOTAL[0])
            pe.wait_ge(x_loaded, 16)
            pe.wait_ge(consts, 4)
            pe.wait_ge(started, 2)

            def transpose_norm(K, g, w):
                pe.wait_ge(xn_done.sem, xn_done.at(K, g, w + 1))
                rows = xn2 if K and w == LN2 else xn
                for t in range(T):
                    mm = pe.transpose(D[:, t * P:(t + 1) * P], rows[:, t, :], ident)
                mm.then_inc(xnT_psum.sem, 1)

            def project(K, g, groups_in):
                pe.wait_ge(xnT_done.sem, xnT_done.at(K, g, LN1 + 1))
                if K == 0:
                    pe.matmul(D[0:HID0, :], wv0[:, :], xnT[:, :], start=True, stop=True).then_inc(proj.sem, 1)
                    pe.wait_ge(ctx_loaded, groups_in)
                    pe.sem_inc(alone, 1)
                    pe.matmul(A[0:HID0, :], wt0[:, :], ctxT[:, :], start=True, stop=True).then_inc(proj.sem, 1)
                    return
                pe.matmul(D[:, :], wq[:, K - 1, :], xnT[:, :], start=True, stop=True).then_inc(proj.sem, 1)
                pe.wait_ge(ctx_loaded, groups_in)
                pe.matmul(A[:, :], wk[:, K - 1, :], ctxT[:, :], start=True, stop=True).then_inc(proj.sem, 1)
                for t in range(T):
                    mm = pe.matmul(B4[:, t, :], ctxT[:, t * P:(t + 1) * P], wv[:, K - 1, :], start=True, stop=True)
                mm.then_inc(proj.sem, 1)

            def cosine_products(K, g):
                pe.wait_ge(proj_read.sem, proj_read.at(K, g, 4))
                pe.sem_inc(alone, 1)
                for j, sq in ((0, vsq), (T, tsq)):
                    for t in range(T):
                        mm = pe.matmul(B[:, j + t:j + t + 1], sq[:, t * P:(t + 1) * P], ones[0:HID0, 0:1],
                                       start=True, stop=True)
                mm.then_inc(cos_psum.sem, 1)
                for t in range(T):
                    mm = pe.matmul(A4[:, t, :], vT[:, t * P:(t + 1) * P], tT[:, t * P:(t + 1) * P],
                                   start=True, stop=True)
                mm.then_inc(cos_psum.sem, 1)

            def spread_norms(K, g):
                pe.wait_ge(norm_pool.sem, norm_pool.at(K, g, 2))
                pe.matmul(D[:, :], ones[:, :], diag.rearrange("p t d -> p (t d)"), start=True, stop=True)\
                    .then_inc(cos_psum.sem, 1)

            def scores(K, g, q):
                if K == 1:
                    pe.wait_ge(proj_read.sem, proj_read.at(K, g, 2))
                    for t in range(T):
                        c = slice(t * P, (t + 1) * P)
                        mm = pe.matmul(A4[:, t, :], qT[:, c], kT[:, c], start=True, stop=True)
                    mm.then_inc(score.sem, 1)
                    return
                t, j = q // 4, q % 4
                if q == 0:
                    pe.wait_ge(proj_read.sem, proj_read.at(K, g, 2))
                    pe.wait_ge(kv_read.sem, kv_read.at(K, g, 1))
                elif q > 1:
                    pe.wait_ge(exp_done.sem, exp_done.at(K, g, q - 1))
                c, r = slice(t * P, (t + 1) * P), slice(32 * j, 32 * j + 32)
                pe.matmul(scores_in[q % 2], qT[r, c], kbd[r, :, c], start=True, stop=True).then_inc(score.sem, 1)

            def transpose_probs(K, g, q):
                if K > 1:
                    pe.wait_ge(prob_done.sem, prob_done.at(K, g, q + 1))
                else:
                    pe.wait_ge(exp_done.sem, exp_done.at(K, g, q + 1))
                if K > 1 and q == 0:
                    pe.wait_ge(proj_read.sem, proj_read.at(K, g, 2))
                elif K == 1:
                    pe.wait_ge(kv_read.sem, kv_read.at(K, g, 1))
                elif q % 2:
                    pe.wait_ge(probT_dve.sem, probT_dve.at(K, g, (q + 1) // 2))
                else:
                    pe.wait_ge(probT_act.sem, probT_act.at(K, g, q // 2))
                for t in range(T):
                    mm = pe.transpose(B4[:, t, :], prob[:, q % 2, t, :], ident)
                mm.then_inc(probT_psum.sem, 1)

            def weigh_values(K, g, q):
                if K == 1:
                    pe.wait_ge(probT_dve.sem, probT_dve.at(K, g, 1))
                    for t in range(T):
                        mm = pe.matmul(D4[:, t, :], probT[:, 0, t, :], val[:, t, :], start=True, stop=True)
                    mm.then_inc(av_done.sem, 1)
                    return
                t, j = q // 4, q % 4
                if q % 2:
                    pe.wait_ge(probT_act.sem, probT_act.at(K, g, q // 2 + 1))
                else:
                    pe.wait_ge(probT_dve.sem, probT_dve.at(K, g, q // 2 + 1))
                if j == 0 and t:
                    pe.wait_ge(ao_done.sem, ao_done.at(K, g, t))
                r = slice(32 * j, 32 * j + 32)
                mm = pe.matmul(D[r, :], va[:, t, r], probT[:, q % 2, :, :].rearrange("p i q -> p (i q)"),
                               start=True, stop=True)
                if j == 3:
                    mm.then_inc(av_done.sem, 1)

            def project_out(K, g):
                pe.wait_ge(aoT_done.sem, aoT_done.at(K, g, T))
                for t in range(T):
                    mm = pe.matmul(A4[:, t, :], aoT[:, t * P:(t + 1) * P], wo[:, K - 2, :], start=True, stop=True)
                mm.then_inc(wo_done.sem, 1)

            def route(K, g):
                pe.wait_ge(xnT_done.sem, xnT_done.at(K, g, LN2 + 1))
                for t in range(T):
                    mm = pe.matmul(B[:, t * EXPERTS:(t + 1) * EXPERTS], xnT[:, t * P:(t + 1) * P], wr[:, K, :],
                                   start=True, stop=True)
                mm.then_inc(logits.sem, 1)

            def places(K, g):
                pe.wait_ge(mask_done.sem, mask_done.at(K, g, 1))
                if K == 2:
                    pe.wait_ge(x2T_done.sem, x2T_done.at(K, g, 1))
                pe.sem_inc(alone, 1)
                pe.matmul(D[:, 0:T * EXPERTS], earlier, mask[:, :, :].rearrange("p t e -> p (t e)"),
                          start=True, stop=True, skip_group_check=True)
                for t in range(T):
                    mm = pe.matmul(D[:, (t + 1) * EXPERTS:(T + 1) * EXPERTS].rearrange("p (u e) -> p u e", e=EXPERTS),
                                   ones[:, :], mask[:, t, :].unsqueeze(1).to_broadcast([P, T - t, EXPERTS]),
                                   start=False, stop=True, skip_group_check=True)
                mm.then_inc(place_psum.sem, 1)

            def pre(K, g, p):
                if K == 4:
                    return
                if p == 1:
                    transpose_norm(K, g, LN1)
                if p == 2:
                    project(K, g, 16 * (g + (GROUPS * K + 1)))
                if K == 0:
                    if p == 3:
                        cosine_products(K, g)
                    if p == 5:
                        spread_norms(K, g)
                elif K == 1:
                    if p == 3:
                        scores(K, g, 0)
                    if p == 4:
                        transpose_probs(K, g, 0)
                    if p == 5:
                        weigh_values(K, g, 0)
                else:
                    if p == 3:
                        scores(K, g, 0)
                    if 0 <= p - 5 < QUADS:
                        transpose_probs(K, g, p - 5)
                    if 0 <= p - 6 < QUADS:
                        weigh_values(K, g, p - 6)
                    if p == 22:
                        project_out(K, g)
                n = NORM2[K]
                if p == n + 1:
                    transpose_norm(K, g, LN2)
                if p == n + 2:
                    route(K, g)
                    if K == 0:
                        pe.matmul(A[0:ACTOR, :], aw1[:, :], xnT[:, :], start=True, stop=True)\
                            .then_inc(act1_psum.sem, 1)
                if K == 0 and p == n + 5:
                    pe.wait_ge(act_dve.sem, act_dve.at(K, g, 2))
                    pe.sem_inc(alone, 1)
                    for t in range(T):
                        mm = pe.matmul(B[:, 64 + t * MAX_K:64 + (t + 1) * MAX_K], aa[:, t * P:(t + 1) * P],
                                       aw2[:, :], start=True, stop=True)
                    mm.then_inc(act2_psum.sem, 1)
                if K and p == n + 5:
                    places(K, g)

            def up_product(g, i):
                if i == 0:
                    pe.wait_ge(x2T_done.sem, x2T_done.at(0, g, 1))
                for which, w, ready in ((0, wg, g_ready), (1, wu, u_ready)):
                    b, turn = up_bank(0, i, which)
                    pe.wait_ge(up_read[b].sem, up_read[b].at(0, g, turn))
                    pe.matmul(up[b][0:ROWS[0], :], w[0][:, i, :], x2T[:, g % 2, :], start=True, stop=True)\
                        .then_inc(ready.sem, 1)

            def down_product(g, i):
                rows, e, c = ROWS[0], i // PER_UNIT[0], i % PER_UNIT[0]
                pe.wait_ge(hid_ready.sem, hid_ready.at(0, g, i + 1))
                if c == 0:
                    pe.wait_ge(y_read.sem, y_read.at(0, g, e))
                for t in range(T):
                    mm = pe.matmul(Y4[:, t, :], hid[0:rows, i % HRING, t * P:(t + 1) * P], wd[0][0:rows, i, :],
                                   start=(c == 0 and t == 0), stop=(c == PER_UNIT[0] - 1), skip_group_check=True)
                if c == PER_UNIT[0] - 1:
                    mm.then_inc(y_ready.sem, 1)

            def trip(g, K, gp):
                for chunks, phases in slots(0, K):
                    for i in chunks:
                        up_product(g, i)
                        if i >= LAG:
                            down_product(g, i - LAG)
                    for p in phases:
                        pre(K, gp, p)
                for i in range(CHUNKS[0] - LAG, CHUNKS[0]):
                    down_product(g, i)

            def before_block(b, K, g0, L):
                if L is not None:
                    pe.wait_ge(table_done.sem, table_done.at(b, 0, 1))
                for layer, first_block in ((1, 1), (2, 2), (3, 5)):
                    if b == first_block:
                        pe.wait_ge(w_loaded[layer], W_TOTAL[layer])

            def expert_of(b, i, j):
                if tile_layer(b, j)[1]:
                    return EXPERTS
                return pe.value_load(table[0:1, b % 2, 0, bass.ds(i * QUOTA + j, 1)], min_val=0, max_val=EXPERTS - 1)

            def chunk(w, e, n, c):
                return w[:, e * n + c, :]

            def chunks_of(w, e, n):
                if isinstance(e, int):
                    return w[:, e * n:(e + 1) * n, :].rearrange("p c r -> p (c r)")
                return w[:, bass.ds(e * n, n), :].rearrange("p c r -> p (c r)")

            def transpose_rows(b, i, j):
                if j:
                    pe.wait_ge(xsT_done.sem, xsT_done.at(b, i, j))
                else:
                    pe.wait_ge(tile_y_read.sem, tile_y_read.at(b, i, 0))
                pe.wait_ge(xs_loaded[j % RING].sem, xs_loaded[j % RING].at(b, i, 16 * (j // RING + 1)))
                pe.transpose(XT, xs[:, j % RING, :], ident).then_inc(xsT_psum.sem, 1)

            tile_expert = {}

            def tile_up(b, i, j, g):
                L, shared = tile_layer(b, j)
                e, n = expert_of(b, i, j), HIDDEN[L] // P
                tile_expert[j] = e
                if shared:
                    t = j - routed[b]
                    if t == 0:
                        pe.wait_ge(x2T_done.sem, x2T_done.at(2, g, 1))
                    rows = x2T[:, 0, t * P:(t + 1) * P]
                else:
                    pe.wait_ge(xsT_done.sem, xsT_done.at(b, i, j + 1))
                    rows = xsT[:, j % 2, :]
                one = L != 2 and j > 0
                pe.wait_ge(tile_h.sem, tile_h.at(b, i, j - 1 if one else j))
                bank_g = up_of(b, j)
                pe.matmul(bank_g[:, 0:HIDDEN[L]], rows, chunks_of(wg[L], e, n), start=True, stop=True)\
                    .then_inc(tile_g.sem, 1)
                if L == 2:
                    pe.matmul(U[:, :], rows, chunks_of(wu[L], e, n), start=True, stop=True).then_inc(tile_u.sem, 1)

            def transpose_hidden(b, i, j):
                L, shared = tile_layer(b, j)
                pe.wait_ge(tile_h.sem, tile_h.at(b, i, j + 1))
                for c in range(HIDDEN[L] // P):
                    mm = pe.transpose(TH[:, c * P:(c + 1) * P], hs[:, j % 2, c * P:(c + 1) * P], ident)
                mm.then_inc(hT_psum.sem, 1)

            def tile_down(b, i, j):
                L, shared = tile_layer(b, j)
                e, n = tile_expert[j], HIDDEN[L] // P
                pe.wait_ge(hT_done.sem, hT_done.at(b, i, j + 1))
                pe.wait_ge(tile_y_read.sem, tile_y_read.at(b, i, j))
                if j + DEPTH <= routed[b]:
                    pe.wait_ge(xsT_done.sem, xsT_done.at(b, i, j + DEPTH))
                for c in range(n):
                    mm = pe.matmul(YT, hsT[:, j % 2, c * P:(c + 1) * P], chunk(wd[L], e, n, c),
                                   start=(c == 0), stop=(c == n - 1))
                mm.then_inc(tile_y.sem, 1)

            def step(b, i, K, g, last):
                for turns, phases in step_slots(b):
                    for p in phases:
                        if K in (2, 3) and 0 < p - 3 < QUADS:
                            scores(K, g, p - 3)
                    attention = K in (2, 3) and BLOCKS[b][2] == 2 and any(4 <= p < 22 for p in phases)
                    if attention:
                        for p in phases:
                            pre(K, g, p)
                    for n in turns:
                        start, up_, hidden_, down = staged(b, n)
                        if down is not None:
                            tile_down(b, i, down)
                        if start is not None and start < routed[b]:
                            transpose_rows(b, i, start)
                        if hidden_ is not None:
                            transpose_hidden(b, i, hidden_)
                        if up_ is not None:
                            tile_up(b, i, up_, g)
                    if not attention:
                        for p in phases:
                            pre(K, g, p)

            run(lambda: first_group(pe, pre), trip, before_block, step, pe)

        @block.scalar
        def _(act):
            act.wait_ge(w_loaded[0], W_TOTAL[0])
            for K in (1, 2, 3):
                scale = float(P) ** -0.5 if K == 1 else float(HD) ** -0.5
                ins = act.activation(bqs[:, K - 1:K], bq[:, K - 1:K], ACT.Copy, scale=scale)
            ins.then_inc(started, 1)
            act.wait_ge(started, 2)

            def evacuate_norm(K, g, w):
                act.wait_ge(xnT_psum.sem, xnT_psum.at(K, g, w + 1))
                act.activation(xnT[:, :], D[:, :], ACT.Copy).then_inc(xnT_done.sem, 1)
                if w == LN2 and K in (0, 2):
                    slot = g % 2 if K == 0 else 0
                    act.activation(x2T[:, slot, :], D[:, :], ACT.Copy).then_inc(x2T_done.sem, 1)

            def read_projections(K, g):
                act.wait_ge(proj.sem, proj.at(K, g, 1))
                if K == 0:
                    act.activation(vT, D[0:HID0, :], ACT.Identity, bias=bv0[:, 0:1]).then_inc(proj_read.sem, 1)
                    act.activation(vsq, D[0:HID0, :], ACT.Square, bias=bv0[:, 0:1]).then_inc(proj_read.sem, 1)
                    act.wait_ge(proj.sem, proj.at(K, g, 2))
                    act.activation(tT, A[0:HID0, :], ACT.Copy).then_inc(proj_read.sem, 1)
                    act.activation(tsq, A[0:HID0, :], ACT.Square).then_inc(proj_read.sem, 1)
                    return
                scale = float(P) ** -0.5 if K == 1 else float(HD) ** -0.5
                act.activation(qT[:, :], D[:, :], ACT.Identity, bias=bqs[:, K - 1:K], scale=scale)\
                    .then_inc(proj_read.sem, 1)
                if K == 1:
                    act.wait_ge(proj.sem, proj.at(K, g, 2))
                    act.activation(kT, A[:, :], ACT.Copy).then_inc(proj_read.sem, 1)
                else:
                    act.wait_ge(proj.sem, proj.at(K, g, 3))
                    act.activation(va[:, :, :], B4[:, :, :], ACT.Copy).then_inc(proj_read.sem, 1)

            def exponentials(K, g, q):
                if K > 1 and q > 1:
                    act.wait_ge(probT_psum.sem, probT_psum.at(K, g, q - 1))
                act.wait_ge(nmax_done.sem, nmax_done.at(K, g, q + 1))
                for i in range(T):
                    if K == 1:
                        ins = act.activation(prob[:, 0, i, :], A4[:, i, :], ACT.Exp, bias=nmax[:, 0, i:i + 1],
                                             accum_out=sums[:, 0, i:i + 1])
                    else:
                        ins = act.activation(prob[:, q % 2, i, :], scores_in[q % 2][:, i, :], ACT.Exp,
                                             bias=nmax[:, q % 2, i:i + 1], accum_out=sums[:, q % 2, i:i + 1])
                ins.then_inc(exp_done.sem, 1)

            def evacuate_probs(K, g, q):
                act.wait_ge(probT_psum.sem, probT_psum.at(K, g, q + 1))
                act.activation(probT[:, q % 2, :, :], B4[:, :, :], ACT.Copy).then_inc(probT_act.sem, 1)

            def pre(K, g, p):
                if K == 4:
                    return
                n = NORM2[K]
                if p == 2:
                    evacuate_norm(K, g, LN1)
                if p == 3:
                    read_projections(K, g)
                if K == 1 and p == 4:
                    exponentials(K, g, 0)
                if K > 1:
                    if 0 <= p - 6 < QUADS and (p - 6) % 2:
                        evacuate_probs(K, g, p - 6)
                    if 0 <= p - 3 < QUADS:
                        exponentials(K, g, p - 3)
                if p == n + 2:
                    evacuate_norm(K, g, LN2)
                if p == n + 4:
                    act.wait_ge(dl_done.sem, dl_done.at(K, g, 1))
                    act.activation(ex[:, :, :], dl[:, :, :], ACT.Exp).then_inc(ex_done.sem, 1)
                if K == 0 and p == n + 3:
                    act.wait_ge(act1_psum.sem, act1_psum.at(K, g, 1))
                    act.activation(ay, A[0:ACTOR, :], ACT.Identity, bias=ab1[:, 0:1]).then_inc(act1.sem, 1)
                if K == 0 and p == n + 5:
                    act.wait_ge(act_pool.sem, act_pool.at(K, g, 2))
                    act.activation(ath, ay2, ACT.Tanh, scale=GELU_A).then_inc(act1.sem, 1)
            def hidden(g, i):
                rows = ROWS[0]
                b, turn = up_bank(0, i)
                act.wait_ge(g_ready.sem, g_ready.at(0, g, i + 1))
                act.wait_ge(hid_ready.sem, hid_ready.at(0, g, i - 1))
                act.activation(tg[0:rows, i % 2, :], up[b][0:rows, :], ACT.Tanh, scale=0.5)\
                    .then_inc(t_ready.sem, 1)
                b, turn = up_bank(0, i, 1)
                act.wait_ge(u_ready.sem, u_ready.at(0, g, i + 1))
                act.activation(uc[0:rows, i % 2, :], up[b][0:rows, :], ACT.Copy).then_inc(up_read[b].sem, 1)

            def trip(g, K, gp):
                for chunks, phases in slots(0, K):
                    for p in phases:
                        pre(K, gp, p)
                    for i in chunks:
                        hidden(g, i)

            def tile_hidden(b, i, j):
                L, shared = tile_layer(b, j)
                if L == 3:
                    act.wait_ge(tile_b.sem, tile_b.at(b, i, j + 1))
                    act.activation(hs[:, j % 2, 0:HIDDEN[L]], tg[:, j % 2, 0:HIDDEN[L]], ACT.Relu).then_inc(tile_h.sem, 1)
                    return
                act.wait_ge(tile_g.sem, tile_g.at(b, i, j + 1))
                if L == 2:
                    act.activation(tg[:, j % 2, :], G[:, :], ACT.Tanh, scale=0.5).then_inc(tile_t.sem, 1)
                else:
                    act.activation(hs[:, j % 2, :], up_of(b, j)[:, :], ACT.Relu).then_inc(tile_h.sem, 1)

            def step(b, i, K, g, last):
                for turns, phases in step_slots(b):
                    for p in phases:
                        pre(K, g, p)
                    for n in turns:
                        start, up_, hidden_, down = staged(b, n)
                        if hidden_ is not None and tile_layer(b, hidden_)[0] == 2:
                            act.wait_ge(hT_psum.sem, hT_psum.at(b, i, hidden_ + 1))
                            act.activation(hsT[:, hidden_ % 2, :], TH[:, :], ACT.Copy).then_inc(hT_done.sem, 1)
                        if up_ is not None:
                            tile_hidden(b, i, up_)

            run(lambda: first_group(act, pre), trip, lambda *block: None, step, act)

        @block.vector
        def _(dve):
            dve.memset(ctxT[C:C + 1, :], 1.0).then_inc(started, 1)
            dve.wait_ge(started, 2)
            dve.wait_ge(w_loaded[0], W_TOTAL[0])
            dve.wait_ge(x_loaded, 16)
            dve.wait_ge(consts, 4)
            dve.tensor_copy(next_row[:, :], list_start)

            def norm_moments(K, g, w):
                if w == LN1 and K == 1:
                    dve.wait_ge(x_added.sem, x_added.at(0, g, EXPERTS))
                if w == LN1 and K > 1:
                    dve.wait_ge(combined.sem, combined.at(K, g, 1))
                if w == LN2:
                    dve.wait_ge(resid.sem, resid.at(K, g, 1))
                dve.wait_ge(mom_done.sem, mom_done.at(K, g, w))
                dve.sem_inc(alone, 1)
                for t in range(T):
                    ins = dve.bn_stats(stats[:, t, :], x[:, g, t, :])
                ins.then_inc(stats_done.sem, 1)
                dve.wait_ge(stats_done.sem, stats_done.at(K, g, w + 1))
                dve.sem_inc(alone, 1)
                for t in range(T):
                    ins = dve.bn_aggr(moments[:, t, :], stats[:, t, :])
                ins.then_inc(mom_done.sem, 1)

            def normalize(K, g, w):
                dve.wait_ge(rstd_done.sem, rstd_done.at(K, g, w + 1))
                rows = xn2 if K and w == LN2 else xn
                if K and w == LN2 and not (K == 1 and isinstance(g, int) and g == 0):
                    dve.wait_ge(scattered.sem, scattered.at(K, g, 0))
                for t in range(T):
                    ins = dve.tensor_scalar(rows[:, t, :], x[:, g, t, :], moments[:, t, 0:1], rstd[:, t:t + 1],
                                            ALU.subtract, ALU.mult)
                ins.then_inc(xn_done.sem, 1)

            def cosine(K, g, p):
                if p == 4:
                    dve.wait_ge(cos_psum.sem, cos_psum.at(K, g, 1))
                    dve.tensor_copy(norm2[:, :], B[:, 0:2 * T]).then_inc(norm_read.sem, 1)
                if p == 6:
                    dve.wait_ge(cos_psum.sem, cos_psum.at(K, g, 3))
                    for t in range(T):
                        ins = dve.tensor_scalar(den[:, t, :], D4[:, t, :], norm[:, t:t + 1], COS_EPS,
                                                ALU.mult, ALU.max)
                    ins.then_inc(cos_dve.sem, 1)
                    dve.wait_ge(cos_dve.sem, cos_dve.at(K, g, 1))
                    dve.reciprocal(rden, den).then_inc(cos_dve.sem, 1)
                    dve.wait_ge(cos_dve.sem, cos_dve.at(K, g, 2))
                    dve.tensor_tensor(tmp[:, :, :], A4[:, :, :], rden, ALU.mult).then_inc(cos_dve.sem, 1)
                    dve.wait_ge(cos_dve.sem, cos_dve.at(K, g, 3))
                    dve.tensor_tensor(x[:, g, :, :], x[:, g, :, :], tmp[:, :, :], ALU.add).then_inc(resid.sem, 1)

            def read_keys_values(K, g):
                if K == 1:
                    dve.wait_ge(proj.sem, proj.at(K, g, 3))
                    dve.tensor_copy(val, B4[:, :, :]).then_inc(kv_read.sem, 1)
                    return
                dve.wait_ge(proj.sem, proj.at(K, g, 2))
                for i in range(4):
                    ins = dve.tensor_scalar(kbd[:, i, :], A[:, :], head_mask[:, i:i + 1], None, ALU.mult)
                ins.then_inc(kv_read.sem, 1)

            def score_max(K, g, q):
                dve.wait_ge(score.sem, score.at(K, g, q + 1))
                dve.tensor_reduce(nmax[:, q % 2, :], scores_in[q % 2], AX.X, ALU.max, negate=True)\
                    .then_inc(nmax_done.sem, 1)

            def evacuate_probs(K, g, q):
                dve.wait_ge(probT_psum.sem, probT_psum.at(K, g, q + 1))
                dve.tensor_copy(probT[:, q % 2, :, :], B4[:, :, :]).then_inc(probT_dve.sem, 1)

            def norm_probs(K, g, q):
                r = slice(T * (q % 2), T * (q % 2) + 4)
                dve.wait_ge(exp_done.sem, exp_done.at(K, g, q + 1))
                dve.reciprocal(rsum[:, r], sums[:, q % 2, :]).then_inc(rsum_done.sem, 1)
                dve.wait_ge(rsum_done.sem, rsum_done.at(K, g, q + 1))
                dve.tensor_tensor(prob[:, q % 2, :, :], prob[:, q % 2, :, :],
                                  rsum[:, r].unsqueeze(2).to_broadcast([P, 4, P]), ALU.mult).then_inc(prob_done.sem, 1)

            def pick_heads(K, g, t):
                dve.wait_ge(av_done.sem, av_done.at(K, g, t + 1))
                if t:
                    dve.wait_ge(aoT_done.sem, aoT_done.at(K, g, t))
                dve.tensor_tensor(ao[:, :, :], D4[:, :, :], head_mask.unsqueeze(2).to_broadcast([P, 4, P]),
                                  ALU.mult).then_inc(ao_done.sem, 1)
                dve.wait_ge(ao_done.sem, ao_done.at(K, g, t + 1))
                dve.tensor_reduce(aoT[:, t * P:(t + 1) * P], ao[:, :, :].rearrange("p i q -> p q i"), AX.X, ALU.add)\
                    .then_inc(aoT_done.sem, 1)

            def add_attention1(K, g):
                dve.wait_ge(av_done.sem, av_done.at(K, g, 1))
                dve.reciprocal(rsum[:, 0:T], sums[:, 0, :]).then_inc(rsum_done.sem, 1)
                dve.wait_ge(rsum_done.sem, rsum_done.at(K, g, 1))
                dve.tensor_tensor(tmp[:, :, :], D4[:, :, :], rsum[:, 0:T].unsqueeze(2).to_broadcast([P, T, P]),
                                  ALU.mult).then_inc(ao_done.sem, 1)
                dve.wait_ge(ao_done.sem, ao_done.at(K, g, 1))
                dve.tensor_tensor(x[:, g, :, :], x[:, g, :, :], tmp[:, :, :], ALU.add).then_inc(resid.sem, 1)

            def gate_start(K, g):
                dve.wait_ge(logits.sem, logits.at(K, g, 1))
                lgp = B[:, 0:T * EXPERTS].rearrange("p (t e) -> p t e", t=T)
                if K == 3:
                    dve.tensor_tensor(lg[:, :, :], lgp, br3[:, :].unsqueeze(1).to_broadcast([P, T, EXPERTS]),
                                      ALU.add).then_inc(lg_done.sem, 1)
                else:
                    dve.tensor_copy(lg[:, :, :], lgp).then_inc(lg_done.sem, 1)
                dve.wait_ge(lg_done.sem, lg_done.at(K, g, 1))
                full = [P, T, EXPERTS, EXPERTS]
                other = lg[:, :, :].unsqueeze(2).to_broadcast(full)
                own = lg[:, :, :].unsqueeze(3).to_broadcast(full)
                dve.tensor_tensor(gt[:, :, :, :], other, own, ALU.is_gt)
                dve.tensor_tensor(eq[:, :, :, :], other, own, ALU.is_equal).then_inc(compared.sem, 1)
                dve.tensor_reduce(nlmax[:, :], lg[:, :, :], AX.X, ALU.max).then_inc(gstep.sem, 1)
                dve.wait_ge(gstep.sem, gstep.at(K, g, 1))
                dve.tensor_tensor(dl[:, :, :], lg[:, :, :], nlmax[:, :].unsqueeze(2).to_broadcast([P, T, EXPERTS]),
                                  ALU.subtract).then_inc(dl_done.sem, 1)

            def find_k(K, g):
                dve.wait_ge(act2_psum.sem, act2_psum.at(K, g, 1))
                alp = B[:, 64:64 + T * MAX_K].rearrange("p (t k) -> p t k", t=T)
                wide = [P, T, MAX_K]
                dve.scalar_tensor_tensor(out=al[:, :, :], in0=alp, scalar=0.5,
                                         in1=ab2[:, :].unsqueeze(1).to_broadcast(wide),
                                         op0=ALU.mult, op1=ALU.add).then_inc(gstep.sem, 1)
                dve.wait_ge(gstep.sem, gstep.at(K, g, 3))
                dve.tensor_scalar(al[:, :, :], al[:, :, :], 30.0, -30.0, ALU.min, ALU.max).then_inc(gstep.sem, 1)
                dve.wait_ge(gstep.sem, gstep.at(K, g, 4))
                dve.tensor_reduce(amax[:, :], al[:, :, :], AX.X, ALU.max).then_inc(gstep.sem, 1)
                dve.wait_ge(gstep.sem, gstep.at(K, g, 5))
                dve.tensor_tensor(aeq[:, :, :], al[:, :, :], amax[:, :].unsqueeze(2).to_broadcast(wide),
                                  ALU.is_ge).then_inc(gstep.sem, 1)
                dve.wait_ge(gstep.sem, gstep.at(K, g, 6))
                dve.scalar_tensor_tensor(out=al[:, :, :], in0=aeq[:, :, :], scalar=-64.0,
                                         in1=iota1.unsqueeze(1).to_broadcast(wide),
                                         op0=ALU.mult, op1=ALU.add).then_inc(gstep.sem, 1)
                dve.wait_ge(gstep.sem, gstep.at(K, g, 7))
                dve.tensor_reduce(kk[:, :], al[:, :, :], AX.X, ALU.min).then_inc(gstep.sem, 1)
                dve.wait_ge(gstep.sem, gstep.at(K, g, 8))
                dve.scalar_tensor_tensor(out=wsel[:, :, :], in0=rank[:, :, :], scalar=-64.0,
                                         in1=kk[:, :].unsqueeze(2).to_broadcast([P, T, EXPERTS]),
                                         op0=ALU.add, op1=ALU.is_lt).then_inc(gstep.sem, 1)

            def gate_finish(K, g):
                wide = [P, T, EXPERTS]
                k = 9 if K == 0 else 2
                dve.wait_ge(gstep.sem, gstep.at(K, g, k))
                if K == 0:
                    dve.wait_ge(ex_done.sem, ex_done.at(K, g, 1))
                    dve.tensor_tensor(wsel[:, :, :], wsel[:, :, :], ex[:, :, :], ALU.mult).then_inc(gstep.sem, 1)
                else:
                    dve.wait_ge(ex_done.sem, ex_done.at(K, g, 1))
                    dve.scalar_tensor_tensor(out=wsel[:, :, :], in0=rank[:, :, :], scalar=2.0, in1=ex[:, :, :],
                                             op0=ALU.is_lt, op1=ALU.mult).then_inc(gstep.sem, 1)
                dve.wait_ge(gstep.sem, gstep.at(K, g, k + 1))
                dve.tensor_reduce(gsum[:, :], (wsel if K % 2 else ex)[:, :, :], AX.X, ALU.add)\
                    .then_inc(gstep.sem, 1)
                dve.wait_ge(gstep.sem, gstep.at(K, g, k + 2))
                dve.reciprocal(grec[:, :], gsum[:, :]).then_inc(gstep.sem, 1)
                dve.wait_ge(gstep.sem, gstep.at(K, g, k + 3))
                dve.scalar_tensor_tensor(out=gstat[:, :, :] if K else gates[:, g % 2, :, :],
                                         in0=wsel[:, :, :], scalar=GATE_SCALE[K],
                                         in1=grec[:, :].unsqueeze(2).to_broadcast(wide),
                                         op0=ALU.mult, op1=ALU.mult).then_inc(gates_done.sem, 1)

            def rank_sum(K, g):
                dve.wait_ge(rank_pool.sem, rank_pool.at(K, g, 2))
                dve.tensor_reduce(rank[:, :, :].rearrange("p t e -> p (t e)"),
                                  gt[:, :, :, :].rearrange("p t e j -> p (t e) j"), AX.X, ALU.add)\
                    .then_inc(gstep.sem, 1)
                if K:
                    dve.wait_ge(gstep.sem, gstep.at(K, g, 2))
                    dve.tensor_scalar(mask[:, :, :], rank[:, :, :], 2.0, None, ALU.is_lt).then_inc(mask_done.sem, 1)

            def find_rows(K, g):
                dve.wait_ge(place_psum.sem, place_psum.at(K, g, 1))
                wide = [P, T, EXPERTS]
                dve.tensor_tensor(place[:, :, :], D[:, 0:T * EXPERTS].rearrange("p (t e) -> p t e", t=T),
                                  next_row[:, :].unsqueeze(1).to_broadcast(wide), ALU.add).then_inc(rstep.sem, 1)
                dve.wait_ge(rstep.sem, rstep.at(K, g, 1))
                dve.tensor_tensor(next_row[:, :], next_row[:, :], D[:, T * EXPERTS:(T + 1) * EXPERTS], ALU.add)\
                    .then_inc(rstep.sem, 1)
                dve.wait_ge(gates_done.sem, gates_done.at(K, g, 1))
                for s in range(2):
                    dve.scalar_tensor_tensor(out=pick[:, s, :, :], in0=rank[:, :, :], scalar=float(s),
                                             in1=place[:, :, :], op0=ALU.is_equal, op1=ALU.mult)
                    ins = dve.scalar_tensor_tensor(out=pick[:, 2 + s, :, :], in0=rank[:, :, :], scalar=float(s),
                                                   in1=gstat[:, :, :], op0=ALU.is_equal, op1=ALU.mult)
                ins.then_inc(rstep.sem, 1)
                dve.wait_ge(rstep.sem, rstep.at(K, g, 3))
                dve.tensor_reduce(picked[:, :, :].rearrange("p s t -> p (s t)"),
                                  pick[:, :, :, :].rearrange("p s t e -> p (s t) e"), AX.X, ALU.add)\
                    .then_inc(rstep.sem, 1)
                dve.wait_ge(rstep.sem, rstep.at(K, g, 4))
                dve.tensor_copy(routes[:, g, :, :], picked[:, :, :])
                dve.tensor_copy(pos_now[:, :, :], picked[:, 0:2, :]).then_inc(pos_done.sem, 1)

            def recall(K, g):
                dve.wait_ge(combined.sem, combined.at(K, g, 0))
                dve.tensor_copy(gate_back[:, :, :], routes[:, g, 2:4, :])
                dve.tensor_copy(pos_back[:, :, :], routes[:, g, 0:2, :]).then_inc(recalled.sem, 1)

            def combine(K, g):
                for s in range(2):
                    dve.wait_ge(gathered[s].sem, gathered[s].at(K, g, 16 * T))
                    if s:
                        dve.wait_ge(cstep.sem, cstep.at(K, g, 1))
                    for t in range(T):
                        ins = dve.scalar_tensor_tensor(out=x[:, g, t, :], in0=yg[:, s, t, :],
                                                       scalar=gate_back[:, s, t:t + 1], in1=x[:, g, t, :],
                                                       op0=ALU.mult, op1=ALU.add)
                    ins.then_inc((combined if s else cstep).sem, 1)

            def pre(K, g, p):
                n = NORM2[K]
                if K > 1 and p == 0:
                    combine(K, g)
                if K == 4:
                    return
                if p == 0:
                    norm_moments(K, g, LN1)
                if p == 1:
                    normalize(K, g, LN1)
                if K == 0:
                    cosine(K, g, p)
                elif K == 1:
                    if p == 3:
                        read_keys_values(K, g)
                        score_max(K, g, 0)
                    if p == 5:
                        evacuate_probs(K, g, 0)
                    if p == 6:
                        add_attention1(K, g)
                else:
                    if p == 3:
                        read_keys_values(K, g)
                    if 0 <= p - 6 < QUADS and (p - 6) % 2 == 0:
                        evacuate_probs(K, g, p - 6)
                    if 0 <= p - 3 < QUADS:
                        score_max(K, g, p - 3)
                    if 0 <= p - 4 < QUADS:
                        norm_probs(K, g, p - 4)
                    if p >= 10 and (p - 10) % 4 == 0 and (p - 10) // 4 < T:
                        pick_heads(K, g, (p - 10) // 4)
                    if p == 23:
                        dve.wait_ge(wo_done.sem, wo_done.at(K, g, 1))
                        dve.wait_ge(bo_done.sem, bo_done.at(K, g, 1))
                        dve.tensor_tensor(x[:, g, :, :], x[:, g, :, :], A4[:, :, :], ALU.add)\
                            .then_inc(resid.sem, 1)
                if p == n:
                    norm_moments(K, g, LN2)
                if p == n + 1:
                    normalize(K, g, LN2)
                if p == n + 3:
                    gate_start(K, g)
                if p == n + 4:
                    rank_sum(K, g)
                    if K == 0:
                        dve.wait_ge(act_pool.sem, act_pool.at(K, g, 1))
                        dve.tensor_scalar(ay2, ay2, GELU_C, 1.0, ALU.mult, ALU.add).then_inc(act_dve.sem, 1)
                if K == 0 and p == n + 5:
                    dve.wait_ge(act1.sem, act1.at(K, g, 2))
                    dve.scalar_tensor_tensor(out=aa, in0=ath, scalar=1.0, in1=ay, op0=ALU.add, op1=ALU.mult)\
                        .then_inc(act_dve.sem, 1)
                if K == 0 and p == n + 6:
                    find_k(K, g)
                if p == n + (6 if K == 0 else 5):
                    gate_finish(K, g)
                if K and p == n + 6:
                    find_rows(K, g)

            def hidden(g, i):
                rows, (b, turn) = ROWS[0], up_bank(0, i)
                dve.wait_ge(t_ready.sem, t_ready.at(0, g, i + 1))
                dve.scalar_tensor_tensor(out=tg[0:rows, i % 2, :], in0=tg[0:rows, i % 2, :], scalar=1.0,
                                         in1=up[b][0:rows, :], op0=ALU.add, op1=ALU.mult)\
                    .then_inc(up_read[b].sem, 1)

            def weigh_expert(g, e):
                if e == 0:
                    dve.wait_ge(gates_done.sem, gates_done.at(0, g, 1))
                dve.wait_ge(y_ready.sem, y_ready.at(0, g, e + 1))
                dve.wait_ge(x_added.sem, x_added.at(0, g, max(e - 1, 0)))
                dve.tensor_tensor(ytmp[:, e % 2, :, :], Y4[:, :, :],
                                  gates[:, g % 2, :, e].unsqueeze(2).to_broadcast([P, T, P]), ALU.mult)\
                    .then_inc(y_read.sem, 1)

            def trip(g, K, gp):
                if K == 1:
                    dve.wait_ge(zeroed, 16 * len(lists) * (GROUPS - 1))
                for chunks, phases in slots(0, K):
                    for i in chunks:
                        if done_before(0, i) is not None:
                            weigh_expert(g, done_before(0, i))
                        hidden(g, i)
                    for p in phases:
                        pre(K, gp, p)
                for i in range(CHUNKS[0], CHUNKS[0] + LAG):
                    if done_before(0, i) is not None:
                        weigh_expert(g, done_before(0, i))
                weigh_expert(g, EXPERTS - 1)

            def make_table(b):
                def after(k):
                    dve.wait_ge(tstep.sem, tstep.at(b, 0, k))
                per_list = [P, EXPERTS, 16]
                per_tile = [P, MAX_TILES, EXPERTS]
                dve.wait_ge(pos_done.sem, pos_done.at(BLOCKS[b - 1][0], BLOCKS[b - 1][1] + STEPS - 1, 1))
                dve.tensor_tensor(filled[:, :], next_row[:, :], list_start, ALU.subtract).then_inc(tstep.sem, 1)
                after(1)
                dve.tensor_tensor(tcmp, filled[:, :].unsqueeze(2).to_broadcast(per_list),
                                  tile_start.unsqueeze(1).to_broadcast(per_list), ALU.is_gt).then_inc(tstep.sem, 1)
                after(2)
                dve.tensor_reduce(ntile[:, :], tcmp, AX.X, ALU.add).then_inc(tstep.sem, 1)
                after(3)
                dve.tensor_tensor(ncmp, ntile[:, :].unsqueeze(1).to_broadcast([P, EXPERTS, EXPERTS]),
                                  before, ALU.mult).then_inc(tstep.sem, 1)
                after(4)
                dve.tensor_reduce(tprev[:, :], ncmp, AX.X, ALU.add).then_inc(tstep.sem, 1)
                after(5)
                dve.tensor_tensor(tend[:, :], tprev[:, :], ntile[:, :], ALU.add).then_inc(tstep.sem, 1)
                after(6)
                dve.tensor_tensor(jcmp, iota_tile.unsqueeze(2).to_broadcast(per_tile),
                                  tend[:, :].unsqueeze(1).to_broadcast(per_tile), ALU.is_ge).then_inc(tstep.sem, 1)
                after(7)
                dve.tensor_tensor(jcmp2, jcmp, ntile[:, :].unsqueeze(1).to_broadcast(per_tile),
                                  ALU.mult).then_inc(tstep.sem, 1)
                after(8)
                dve.tensor_reduce(tile_e[:, :], jcmp, AX.X, ALU.add)
                dve.tensor_reduce(tile_o[:, :], jcmp2, AX.X, ALU.add).then_inc(tstep.sem, 1)
                after(9)
                dve.tensor_tensor(tile_k[:, :], iota_tile, tile_o[:, :], ALU.subtract).then_inc(tstep.sem, 1)
                after(10)
                dve.scalar_tensor_tensor(out=tile_r[:, :], in0=tile_e[:, :], scalar=float(LIST // P),
                                         in1=tile_k[:, :], op0=ALU.mult, op1=ALU.add).then_inc(tstep.sem, 1)
                after(11)
                dve.tensor_scalar(table[:, b % 2, 0, :], tile_e[:, :], float(EXPERTS - 1), None, ALU.min)
                dve.tensor_scalar(table[:, b % 2, 1, :], tile_r[:, :], float(P), None, ALU.mult)\
                    .then_inc(table_done.sem, 1)

            def before_block(b, K, g0, L):
                if b == 5:
                    dve.wait_ge(w_loaded[3], W_TOTAL[3])
                if K > 1:
                    recall(K, g0)
                if L is not None:
                    make_table(b)
                    dve.tensor_copy(next_row[:, :], list_start)

            expert_of = {}

            def tile_result(b, i, j, g):
                dve.wait_ge(tile_y.sem, tile_y.at(b, i, j + 1))
                if tile_layer(b, j)[1]:
                    t = j - routed[b]
                    dve.scalar_tensor_tensor(out=x[:, g, t, :], in0=YT, scalar=SHARED_GATE,
                                             in1=x[:, g, t, :], op0=ALU.mult, op1=ALU.add)\
                        .then_inc(tile_y_read.sem, 1)
                    return
                r = j % RING
                dve.wait_ge(y_stored[r].sem, y_stored[r].at(b, i, 16 * (j // RING)))
                if tile_layer(b, j)[0] == 3:
                    dve.tensor_tensor(ys[:, r, :], YT, b2_3[:, bass.ds(expert_of[j] * P, P)], ALU.add).then_inc(tile_y_read.sem, 1)
                    return
                dve.tensor_copy(ys[:, r, :], YT).then_inc(tile_y_read.sem, 1)

            def tile_hidden(b, i, j):
                if tile_layer(b, j)[0] == 3:
                    e = expert_of[j] = dve.value_load(table[0:1, b % 2, 0, bass.ds(i * QUOTA + j, 1)], min_val=0, max_val=EXPERTS - 1)
                    dve.wait_ge(tile_g.sem, tile_g.at(b, i, j + 1))
                    dve.tensor_tensor(tg[:, j % 2, 0:HIDDEN[3]], up_of(b, j)[:, 0:HIDDEN[3]],
                                      b1_3[:, bass.ds(e * HIDDEN[3], HIDDEN[3])], ALU.add).then_inc(tile_b.sem, 1)
                    return
                k = pair(b, j) + 1
                dve.wait_ge(tile_t.sem, tile_t.at(b, i, k))
                dve.scalar_tensor_tensor(out=tg[:, j % 2, :], in0=tg[:, j % 2, :], scalar=1.0, in1=G[:, :],
                                         op0=ALU.add, op1=ALU.mult).then_inc(tile_w.sem, 1)
                dve.wait_ge(tile_w.sem, tile_w.at(b, i, k))
                dve.wait_ge(tile_u.sem, tile_u.at(b, i, k))
                dve.tensor_tensor(hs[:, j % 2, :], tg[:, j % 2, :], U[:, :], ALU.mult).then_inc(tile_h.sem, 1)

            def step(b, i, K, g, last):
                def all_phases(phases):
                    for p in phases:
                        pre(K, g, p)
                        if K > 1 and p == (0 if K == 4 else 3) and not last:
                            recall(K, g + 1)

                for turns, phases in step_slots(b):
                    attention = K in (2, 3) and any(3 <= p < 23 for p in phases)
                    if attention:
                        all_phases(phases)
                    for n in turns:
                        start, up_, hidden_, down = staged(b, n)
                        if start is not None and start < routed[b]:
                            dve.wait_ge(xsT_psum.sem, xsT_psum.at(b, i, start + 1))
                            dve.tensor_copy(xsT[:, start % 2, :], XT).then_inc(xsT_done.sem, 1)
                        if down is not None:
                            tile_result(b, i, down, g)
                        if hidden_ is not None and tile_layer(b, hidden_)[0] != 2:
                            w = HIDDEN[tile_layer(b, hidden_)[0]]
                            dve.wait_ge(hT_psum.sem, hT_psum.at(b, i, hidden_ + 1))
                            dve.tensor_copy(hsT[:, hidden_ % 2, 0:w], TH[:, 0:w]).then_inc(hT_done.sem, 1)
                        if up_ is not None and tile_layer(b, up_)[0] != 1:
                            tile_hidden(b, i, up_)
                    if not attention:
                        all_phases(phases)

            run(lambda: first_group(dve, pre), trip, before_block, step, dve)

        @block.gpsimd
        def _(pool):
            pool.memset(ones[:, :], 1.0)
            pool.memset(half[:, 0:8], -0.5)
            pool.memset(half[:, 8:16], 0.5)
            pool.memset(eps[:, :], LN_EPS).then_inc(consts, 1)
            pool.memset(gt[:, :, :, :], 0.0).then_inc(consts, 1)
            pool.memset(zeros, 0.0).then_inc(consts, 1)
            pool.memset(ytmp[:, :, :, :], 0.0).then_inc(consts, 1)
            pool.wait_ge(consts, 4)
            pool.wait_ge(w_loaded[0], W_TOTAL[0])
            pool.wait_ge(x_loaded, 16)

            def inverse_deviation(K, g, w):
                pool.wait_ge(mom_done.sem, mom_done.at(K, g, w + 1))
                pool.tensor_tensor(vare[:, :], moments[:, :, 1], eps[:, :], ALU.add).then_inc(vare_done.sem, 1)
                pool.wait_ge(vare_done.sem, vare_done.at(K, g, w + 1))
                pool.tensor_tensor(rstd[:, :], vare[:, :], half[:, 0:T], ALU.pow).then_inc(rstd_done.sem, 1)

            def norms(K, g):
                pool.wait_ge(norm_read.sem, norm_read.at(K, g, 1))
                pool.tensor_tensor(norm[:, :], norm2[:, :], half[:, 8:8 + 2 * T], ALU.pow).then_inc(norm_pool.sem, 1)
                pool.wait_ge(norm_pool.sem, norm_pool.at(K, g, 1))
                pool.tensor_tensor(diag, ident.unsqueeze(1).to_broadcast([P, T, P]),
                                   norm[:, T:2 * T].unsqueeze(2).to_broadcast([P, T, P]), ALU.mult)\
                    .then_inc(norm_pool.sem, 1)

            def count_before(K, g):
                full = [P, T, EXPERTS, EXPERTS]
                pool.wait_ge(compared.sem, compared.at(K, g, 1))
                pool.tensor_tensor(eq[:, :, :, :], eq[:, :, :, :], before.unsqueeze(1).to_broadcast(full),
                                   ALU.mult).then_inc(rank_pool.sem, 1)
                pool.wait_ge(rank_pool.sem, rank_pool.at(K, g, 1))
                pool.tensor_tensor(gt[:, :, :, :], gt[:, :, :, :], eq[:, :, :, :], ALU.add)\
                    .then_inc(rank_pool.sem, 1)

            def scatter(K, g, block_list):
                pool.wait_ge(pos_done.sem, pos_done.at(K, g, 1))
                pool.sem_inc(alone, 1)
                for s in range(2):
                    for t in range(T):
                        pool.indirect_dma_start(
                            out=block_list[:, :], in_=xn2[:, t, :], in_offset=None,
                            out_offset=bass.IndirectOffsetOnAxis(ap=pos_now[:, s, t:t + 1], axis=0))\
                            .then_inc(scattered.sem, 16)

            def gather(K, g, block_list):
                pool.wait_ge(recalled.sem, recalled.at(K, g, 1))
                pool.sem_inc(alone, 1)
                for s in range(2):
                    for t in range(T):
                        pool.indirect_dma_start(
                            out=yg[:, s, t, :], in_=block_list[:, :], out_offset=None,
                            in_offset=bass.IndirectOffsetOnAxis(ap=pos_back[:, s, t:t + 1], axis=0))\
                            .then_inc(gathered[s].sem, 16)

            def pre(K, g, p):
                if K == 4:
                    return
                n = NORM2[K]
                if p == 0:
                    inverse_deviation(K, g, LN1)
                if K == 0 and p == 4:
                    norms(K, g)
                if K > 1 and p == 2:
                    pool.wait_ge(xn_done.sem, xn_done.at(K, g, 1))
                    pool.sem_inc(alone, 1)
                    pool.tensor_tensor(x[:, g, :, :], x[:, g, :, :],
                                       bo[:, K - 2, :].unsqueeze(1).to_broadcast([P, T, P]), ALU.add)\
                        .then_inc(bo_done.sem, 1)
                if p == n:
                    inverse_deviation(K, g, LN2)
                if p == n + 3:
                    count_before(K, g)
                if K == 0 and p == n + 4:
                    pool.wait_ge(act1.sem, act1.at(K, g, 1))
                    pool.tensor_tensor(ay2, ay, ay, ALU.mult).then_inc(act_pool.sem, 1)
                    pool.wait_ge(act_dve.sem, act_dve.at(K, g, 1))
                    pool.tensor_tensor(ay2, ay2, ay, ALU.mult).then_inc(act_pool.sem, 1)

            def hidden(g, i):
                rows = ROWS[0]
                for which in (0, 1):
                    b, turn = up_bank(0, i, which)
                    pool.wait_ge(up_read[b].sem, up_read[b].at(0, g, turn + 1))
                pool.tensor_tensor(hid[0:rows, i % HRING, :], tg[0:rows, i % 2, :], uc[0:rows, i % 2, :],
                                   ALU.mult).then_inc(hid_ready.sem, 1)

            def add_expert(g, e):
                pool.wait_ge(y_read.sem, y_read.at(0, g, e + 1))
                pool.wait_ge(x_added.sem, x_added.at(0, g, e))
                pool.sem_inc(alone, 1)
                pool.tensor_tensor(x[:, g, :, :], x[:, g, :, :], ytmp[:, e % 2, :, :], ALU.add)\
                    .then_inc(x_added.sem, 1)

            def trip(g, K, gp):
                if K == 1:
                    pool.wait_ge(zeroed, 16 * len(lists) * (GROUPS - 1))
                for chunks, phases in slots(0, K):
                    for i in chunks:
                        if done_before(0, i) is not None:
                            add_expert(g, done_before(0, i))
                        hidden(g, i)
                    for p in phases:
                        pre(K, gp, p)
                        if K == 1 and p == NORM2[K] + 7:
                            scatter(K, gp, lists[0])
                for i in range(CHUNKS[0], CHUNKS[0] + LAG):
                    if done_before(0, i) is not None:
                        add_expert(g, done_before(0, i))
                add_expert(g, EXPERTS - 1)

            def before_block(b, K, g0, L):
                if K > 1:
                    if BLOCKS[b - 1][2] is not None:
                        for stored in y_stored:
                            pool.wait_ge(stored.sem, stored.at(b - 1, STEPS - 1, stored.per[b - 1]))
                    gather(K, g0, lists[(b - 2) % 3])

            def step(b, i, K, g, last):
                for turns, phases in step_slots(b):
                    for p in phases:
                        pre(K, g, p)
                        if K > 1 and p == (0 if K == 4 else 3) and not last:
                            gather(K, g + 1, lists[(b - 2) % 3])
                        if K < 4 and p == NORM2[K] + 7:
                            scatter(K, g, lists[b % 3])

            run(lambda: first_group(pool, pre), trip, before_block, step, pool)


def kernel(**inputs):
    import numpy as np
    import concourse.bacc as bacc
    from concourse.bass_utils import run_bass_kernel_spmd

    a = {k: np.asarray(v) for k, v in inputs.items()}
    ident = np.eye(P, dtype=np.float32)
    head_mask = (np.arange(P)[:, None] // HD % 4 == np.arange(4)[None, :]).astype(np.float32)
    before = np.broadcast_to(np.tril(np.ones((EXPERTS, EXPERTS), np.float32), -1).reshape(1, 64), (P, 64))
    iota1 = np.broadcast_to(np.arange(1, MAX_K + 1, dtype=np.float32)[None, :], (P, MAX_K))
    spread = lambda row: np.broadcast_to(row.astype(np.float32)[None, :], (P, len(row)))
    list_start, tile_start = spread(np.arange(EXPERTS) * LIST), spread(np.arange(LIST // P) * P)
    iota_tile = spread(np.arange(MAX_TILES))
    e, r0 = EXPERTS, ROWS[0]

    def columns(w):
        return w.transpose(1, 0, 2).reshape(P, -1, P)

    def rows(w):
        return w.reshape(-1, P, P).transpose(1, 0, 2)

    host = {
        "const": np.concatenate([ident, head_mask, before, iota1, np.triu(ident * 0 + 1, 1), list_start,
                                 tile_start, iota_tile], axis=1),
        "x": a["x"].reshape(GROUPS, T, P, P),
        "ctxT": a["ctx_768"].reshape(GROUPS, N, C).transpose(0, 2, 1),
        "wv0": a["L0_xattn_Wv"].T, "wt0": a["L0_xattn_Wt"].T,
        "bt0": a["L0_xattn_bt"].reshape(1, HID0), "bv0": a["L0_xattn_bv"].reshape(HID0, 1),
        "aw1": a["L0_ffn_actor_w1"].T, "ab1": a["L0_ffn_actor_b1"].reshape(ACTOR, 1),
        "aw2": a["L0_ffn_actor_w2"].T, "ab2": a["L0_ffn_actor_b2"],
        "wr": np.stack([a["L0_ffn_router_w"].T, a["L1_ffn_Wr"], a["L2_ffn_gate_W"].T, a["L3_ffn_Wr"]], axis=1),
        "br3": a["L3_ffn_br"],
        "bq": np.stack([a[f"L{K}_xattn_bq"] for K in (1, 2, 3)], axis=1),
        "wq": np.stack([a["L1_xattn_Wq"], a["L2_xattn_Wq"], a["L3_xattn_Wq"].T], axis=1),
        "wk": np.stack([a["L1_xattn_Wk"], a["L2_xattn_Wk"], a["L3_xattn_Wk"].T], axis=1),
        "wv": np.stack([a["L1_xattn_Wv"], a["L2_xattn_Wv"], a["L3_xattn_Wv"].T], axis=1),
        "bk": np.stack([a[f"L{K}_xattn_bk"] for K in (1, 2, 3)])[None],
        "bv": np.stack([a[f"L{K}_xattn_bv"] for K in (1, 2, 3)])[None],
        "wo": np.stack([a["L2_xattn_Wo"], a["L3_xattn_Wo"].T], axis=1),
        "bo": np.stack([a["L2_xattn_bo"], a["L3_xattn_bo"]]),
        "wg0": a["L0_ffn_gate_w"].reshape(-1, r0, P).transpose(2, 0, 1),
        "wu0": a["L0_ffn_up_w"].reshape(-1, r0, P).transpose(2, 0, 1),
        "wd0": a["L0_ffn_down_w"].reshape(e, P, PER_UNIT[0], r0).transpose(3, 0, 2, 1).reshape(r0, -1, P),
        "wg1": columns(a["L1_ffn_W1"]), "wd1": rows(a["L1_ffn_W2"]),
        "wg2": np.concatenate([columns(a["L2_ffn_w1_e"]), columns(a["L2_ffn_w1_s"])], axis=1),
        "wu2": np.concatenate([columns(a["L2_ffn_w3_e"]), columns(a["L2_ffn_w3_s"])], axis=1),
        "wd2": np.concatenate([rows(a["L2_ffn_w2_e"]), rows(a["L2_ffn_w2_s"])], axis=1),
        "wg3": columns(a["L3_ffn_W1"]), "wd3": rows(a["L3_ffn_W2"]),
        "b1_3": a["L3_ffn_b1"].reshape(-1), "b2_3": a["L3_ffn_b2"].reshape(-1),
    }
    nc = bacc.Bacc("TRN2", target_bir_lowering=False, num_devices=1)
    arrays, dram = {}, {}
    for name, v in host.items():
        arrays[f"in_{name}"] = np.ascontiguousarray(v)
        dram[name] = nc.dram_tensor(f"in_{name}", v.shape, F32, kind="ExternalInput").ap()
    out = nc.dram_tensor("out_0", (GROUPS, T, P, P), F32, kind="ExternalOutput").ap()
    build(nc, dram, out)
    r = run_bass_kernel_spmd(nc, [arrays], core_ids=[0])
    return r.results[0]["out_0"].reshape(GROUPS * T, P, P)
```
